# Optimizing a Trainium2 kernel written in Bass

```python
import numpy as np
import jax
import jax.numpy as jnp

def _softmax(x, axis=-1):
    return jax.nn.softmax(x, axis=axis)

def _gelu(x):
    return jax.nn.gelu(x, approximate=True)

def _silu(x):
    return jax.nn.silu(x)

def _sigmoid(x):
    return jax.nn.sigmoid(x)

def _layernorm(x, axis=-1, eps=1e-05):
    m = jnp.mean(x, axis=axis, keepdims=True)
    v = jnp.var(x, axis=axis, keepdims=True)
    return (x - m) / jnp.sqrt(v + eps)

def _scatter_add(tgt, idx, src, axis=0):
    return tgt.at[idx].add(src)

def _segment_sum(src, seg, n):
    return jax.ops.segment_sum(src, seg, n)
kernel_name = 'mk_prb_d1_jaxref_r8_8b841f'

def setup_inputs(seed: int=0):
    np.random.seed(seed)
    _w = jnp.asarray

    def _L0_attn_setup():
        import jax, jax.numpy as jnp
        import numpy as np
        DIM = 128
        INNER = DIM // 2
        DSTATE = 8
        KSZ = 3
        DTRANK = max(INNER // 8, 4)
        B, L = (4, 512)

        def _dwconv_silu(u, kern):
            c = u.shape[-1]
            v = jnp.transpose(u, (0, 2, 1))
            v = jax.lax.conv_general_dilated(v, kern, (1,), [(KSZ // 2, KSZ // 2)], dimension_numbers=('NCH', 'OIH', 'NCH'), feature_group_count=c)
            return jax.nn.silu(jnp.transpose(v, (0, 2, 1)))

        def _forward(x, W_in, Kx, Kz, W_xproj, W_dt, b_dt, A_log, D, W_out):
            h = jnp.einsum('bld,ed->ble', x, W_in)
            xb, zb = jnp.split(h, 2, axis=-1)
            xb = _dwconv_silu(xb, Kx)
            zb = _dwconv_silu(zb, Kz)
            proj = jnp.einsum('blc,oc->blo', xb, W_xproj)
            dt_raw = proj[..., :DTRANK]
            b_raw = proj[..., DTRANK:DTRANK + DSTATE]
            c_raw = proj[..., DTRANK + DSTATE:]
            delta = jnp.clip(jax.nn.softplus(jnp.einsum('blr,cr->blc', dt_raw, W_dt) + b_dt), 0.0001, 1.0)
            b_term = jnp.tanh(b_raw)
            c_term = jnp.tanh(c_raw)
            a = jax.nn.softplus(A_log) + 0.0001
            decay = jnp.clip(jnp.exp(-delta[..., None] * a), 0.0001, 1.0)
            drive = (1.0 - decay) * (b_term[:, :, None, :] * xb[..., None])

            def step(state, inp):
                dec_t, drv_t, c_t, x_t = inp
                state = dec_t * state + drv_t
                y = jnp.sum(state * c_t[:, None, :], axis=-1) + D * x_t
                return (state, y)
            tm = lambda t: jnp.moveaxis(t, 1, 0)
            state0 = jnp.zeros((x.shape[0], INNER, DSTATE), dtype=jnp.float32)
            _, ys = jax.lax.scan(step, state0, (tm(decay), tm(drive), tm(c_term), tm(xb)))
            y = jnp.moveaxis(ys, 0, 1)
            return jnp.einsum('bld,ed->ble', jnp.concatenate([y, zb], axis=-1), W_out)
        key = jax.random.key(seed)
        ks = jax.random.split(key, 8)
        s = 0.02
        x = jax.random.normal(ks[0], (B, L, DIM), dtype=jnp.float32)
        W_in = jax.random.normal(ks[1], (DIM, DIM), dtype=jnp.float32) * s
        Kx = jax.random.normal(ks[2], (INNER, 1, KSZ), dtype=jnp.float32) * 0.1
        Kz = jax.random.normal(ks[3], (INNER, 1, KSZ), dtype=jnp.float32) * 0.1
        W_xproj = jax.random.normal(ks[4], (DTRANK + 2 * DSTATE, INNER), dtype=jnp.float32) * s
        W_dt = jax.random.normal(ks[5], (INNER, DTRANK), dtype=jnp.float32) * s
        dt_init = jnp.exp(jnp.linspace(jnp.log(0.02), jnp.log(0.2), INNER))
        b_dt = jnp.log(jnp.expm1(dt_init)).astype(jnp.float32)
        A_log = jnp.log(jnp.tile(jnp.arange(1, DSTATE + 1, dtype=jnp.float32), (INNER, 1)))
        D = jnp.ones((INNER,), dtype=jnp.float32)
        W_out = jax.random.normal(ks[6], (DIM, DIM), dtype=jnp.float32) * s
        return {'x': x, 'W_in': W_in, 'Kx': Kx, 'Kz': Kz, 'W_xproj': W_xproj, 'W_dt': W_dt, 'b_dt': b_dt, 'A_log': A_log, 'D': D, 'W_out': W_out}
    _L0_attn_in = _L0_attn_setup()

    def _L0_ffn_setup():
        import jax, jax.numpy as jnp
        import numpy as np
        TOP_K = 2
        key = jax.random.key(seed)
        k1, k2, k3, k4 = jax.random.split(key, 4)
        B, T, D, H, E = (2, 256, 128, 256, 8)
        x = jax.random.normal(k1, (B, T, D), dtype=jnp.float32)
        w12 = jax.random.normal(k2, (E, 2 * H, D), dtype=jnp.float32) * D ** (-0.5)
        w3 = jax.random.normal(k3, (E, D, H), dtype=jnp.float32) * H ** (-0.5)
        gate_w = jax.random.normal(k4, (E, D), dtype=jnp.float32) * D ** (-0.5)
        return {'x': x, 'w12': w12, 'w3': w3, 'gate_w': gate_w}
    _L0_ffn_in = _L0_ffn_setup()
    _d = {'L0_attn_x': _L0_attn_in['x'], 'L0_attn_W_in': _L0_attn_in['W_in'], 'L0_attn_Kx': _L0_attn_in['Kx'], 'L0_attn_Kz': _L0_attn_in['Kz'], 'L0_attn_W_xproj': _L0_attn_in['W_xproj'], 'L0_attn_W_dt': _L0_attn_in['W_dt'], 'L0_attn_b_dt': _L0_attn_in['b_dt'], 'L0_attn_A_log': _L0_attn_in['A_log'], 'L0_attn_D': _L0_attn_in['D'], 'L0_attn_W_out': _L0_attn_in['W_out'], 'L0_ffn_w12': _L0_ffn_in['w12'], 'L0_ffn_w3': _L0_ffn_in['w3'], 'L0_ffn_gate_w': _L0_ffn_in['gate_w']}
    _x0 = _d['L0_attn_x']
    _d['L0_attn_x'] = jax.random.normal(jax.random.fold_in(jax.random.key(seed), 1), (4, 1024, 128), dtype=_x0.dtype)
    del _x0
    return _d

def reference(L0_attn_x, L0_attn_W_in, L0_attn_Kx, L0_attn_Kz, L0_attn_W_xproj, L0_attn_W_dt, L0_attn_b_dt, L0_attn_A_log, L0_attn_D, L0_attn_W_out, L0_ffn_w12, L0_ffn_w3, L0_ffn_gate_w):

    def _L0_attn_ref(x, W_in, Kx, Kz, W_xproj, W_dt, b_dt, A_log, D, W_out):
        import jax, jax.numpy as jnp
        import numpy as np
        DIM = 128
        INNER = DIM // 2
        DSTATE = 8
        KSZ = 3
        DTRANK = max(INNER // 8, 4)
        B, L = (4, 512)

        def _dwconv_silu(u, kern):
            c = u.shape[-1]
            v = jnp.transpose(u, (0, 2, 1))
            v = jax.lax.conv_general_dilated(v, kern, (1,), [(KSZ // 2, KSZ // 2)], dimension_numbers=('NCH', 'OIH', 'NCH'), feature_group_count=c)
            return jax.nn.silu(jnp.transpose(v, (0, 2, 1)))

        def _forward(x, W_in, Kx, Kz, W_xproj, W_dt, b_dt, A_log, D, W_out):
            h = jnp.einsum('bld,ed->ble', x, W_in)
            xb, zb = jnp.split(h, 2, axis=-1)
            xb = _dwconv_silu(xb, Kx)
            zb = _dwconv_silu(zb, Kz)
            proj = jnp.einsum('blc,oc->blo', xb, W_xproj)
            dt_raw = proj[..., :DTRANK]
            b_raw = proj[..., DTRANK:DTRANK + DSTATE]
            c_raw = proj[..., DTRANK + DSTATE:]
            delta = jnp.clip(jax.nn.softplus(jnp.einsum('blr,cr->blc', dt_raw, W_dt) + b_dt), 0.0001, 1.0)
            b_term = jnp.tanh(b_raw)
            c_term = jnp.tanh(c_raw)
            a = jax.nn.softplus(A_log) + 0.0001
            decay = jnp.clip(jnp.exp(-delta[..., None] * a), 0.0001, 1.0)
            drive = (1.0 - decay) * (b_term[:, :, None, :] * xb[..., None])

            def step(state, inp):
                dec_t, drv_t, c_t, x_t = inp
                state = dec_t * state + drv_t
                y = jnp.sum(state * c_t[:, None, :], axis=-1) + D * x_t
                return (state, y)
            tm = lambda t: jnp.moveaxis(t, 1, 0)
            state0 = jnp.zeros((x.shape[0], INNER, DSTATE), dtype=jnp.float32)
            _, ys = jax.lax.scan(step, state0, (tm(decay), tm(drive), tm(c_term), tm(xb)))
            y = jnp.moveaxis(ys, 0, 1)
            return jnp.einsum('bld,ed->ble', jnp.concatenate([y, zb], axis=-1), W_out)
        return _forward(x, W_in, Kx, Kz, W_xproj, W_dt, b_dt, A_log, D, W_out)

    def _L0_ffn_ref(x, w12, w3, gate_w):
        import jax, jax.numpy as jnp
        import numpy as np
        TOP_K = 2
        E = gate_w.shape[0]
        H = w3.shape[-1]
        scores = jnp.einsum('btd,ed->bte', x, gate_w)
        topk_scores, topk_idx = jax.lax.top_k(scores, TOP_K)
        topk_probs = jax.nn.softmax(topk_scores, axis=-1)
        total_probs = jnp.sum(jax.nn.one_hot(topk_idx, E, dtype=topk_probs.dtype) * topk_probs[..., None], axis=-2)
        h12 = jnp.einsum('btd,ehd->bteh', x, w12)
        h1, h2 = (h12[..., :H], h12[..., H:])
        hidden = jax.nn.silu(h1) * h2
        expert_out = jnp.einsum('bteh,edh->bted', hidden, w3)
        y = jnp.sum(total_probs[..., None] * expert_out, axis=-2)
        return y
    x = L0_attn_x
    xn = _layernorm(x, axis=-1)
    x = x + _L0_attn_ref(xn, L0_attn_W_in, L0_attn_Kx, L0_attn_Kz, L0_attn_W_xproj, L0_attn_W_dt, L0_attn_b_dt, L0_attn_A_log, L0_attn_D, L0_attn_W_out) + _L0_ffn_ref(xn, L0_ffn_w12, L0_ffn_w3, L0_ffn_gate_w)
    return x

_drawn_inputs = setup_inputs


def setup_inputs(seed=0):
    import zlib

    import numpy as np

    out = dict(_drawn_inputs(seed))
    spreads = {'L0_attn_D': (1.0, 0.6)}
    factors = {'L0_attn_W_in': 8.0,
     'L0_attn_Kx': 8.0,
     'L0_attn_Kz': 8.0,
     'L0_attn_W_xproj': 8.0,
     'L0_attn_W_dt': 8.0,
     'L0_attn_b_dt': 8.0,
     'L0_attn_A_log': 8.0,
     'L0_attn_W_out': 8.0}
    for name, (base, spread) in spreads.items():
        noise = np.random.default_rng([zlib.crc32(name.encode()), seed]).standard_normal(out[name].shape)
        drawn = base * np.exp(spread * noise) if base else spread * noise
        out[name] = jnp.asarray(drawn.astype(out[name].dtype))
    for name, factor in factors.items():
        out[name] = (out[name] * factor).astype(out[name].dtype)
    return out
```

```python
from contextlib import ExitStack

import concourse.bass as bass
from concourse import mybir

ALU = mybir.AluOpType
ACT = mybir.ActivationFunctionType
AX_X = mybir.AxisListType.X
F32 = mybir.dt.float32
F32R = mybir.dt.float32r

P = 128
GROUP = 512
TILES = GROUP // P
LN_EPS = 1e-5
CLIP_MIN = 1e-4
A_MIN = 1e-4
PRE_MAX = 20.0
LOWEST = -3.0e38
GATE_STEPS = 16
RSTD_STEPS = 5
MARGIN_STEP = 8


class Stage:

    def __init__(self, sem, per, base=0):
        self.sem, self.per, self.base = sem, per, base

    def at(self, window, done):
        return window * self.per + (self.base + done)


def mixer_moe_kernel(nc, x, w_in_t, conv_taps, wx_bc_t, wx_dt, w_dt_t, b_dt, a_log, d_skip, w_out_y, w_out_yz,
                     w12_t, w3_t, gate_t, select, ident, rank_key, out):
    BATCHES, L, D = x.shape
    GROUPS = L // GROUP
    EXPERTS, H2 = w12_t.shape[1:]
    HB = H2 // 2 // P
    UNITS = EXPERTS
    HALVES = HB
    INNER = w_out_yz.shape[0] // 2
    NJ = a_log.shape[1]
    DTR = wx_dt.shape[0]
    DSTATE = wx_bc_t.shape[1] // 2
    assert D == P and 2 * INNER == P and GROUPS == 2 and HB == 2

    x_v = x.rearrange("b (g t p) d -> b g p t d", g=GROUPS, p=P)
    out_v = out.rearrange("b (g t p) d -> b g p t d", g=GROUPS, p=P)

    with ExitStack() as ctx:
        def sb(name, shape, dt=F32):
            return ctx.enter_context(nc.sbuf_tensor(name, shape, dt))

        def stage(name, per, base=0):
            return Stage(ctx.enter_context(nc.semaphore(name)), per, base)

        def event(name):
            return ctx.enter_context(nc.semaphore(name))

        w12_f = sb("w12_f", [P, EXPERTS, H2])
        w12_hi = sb("w12_hi", [P, EXPERTS, H2], F32R)
        w12_lo = sb("w12_lo", [P, EXPERTS, H2], F32R)
        w3_sb = sb("w3_sb", [P, EXPERTS, HB, D])
        win_f = sb("win_f", [P, P])
        win_hi = sb("win_hi", [P, P], F32R)
        win_lo = sb("win_lo", [P, P], F32R)
        gate_f = sb("gate_f", [P, EXPERTS])
        gate_hi = sb("gate_hi", [P, EXPERTS], F32R)
        gate_lo = sb("gate_lo", [P, EXPERTS], F32R)
        sel_f = sb("sel_f", [P, 2 * NJ, P])
        sel_r = sb("sel_r", [P, 2 * NJ, P], F32R)
        id_sb = sb("id_sb", [P, P])
        key_sb = sb("key_sb", [P, TILES, EXPERTS])
        taps = sb("taps", [P, 3])
        wp = sb("wp", [INNER, P])
        wx_bc_sb = sb("wx_bc_sb", [INNER, 2 * DSTATE])
        wx_dt_sb = sb("wx_dt_sb", [DTR, INNER])
        w_dt_sb = sb("w_dt_sb", [DTR, INNER])
        b_dt_sb = sb("b_dt_sb", [INNER, 1])
        a_in = sb("a_in", [P, NJ])
        a_abs = sb("a_abs", [P, NJ])
        a_exp = sb("a_exp", [P, NJ])
        a_ln = sb("a_ln", [P, NJ])
        a_sum = sb("a_sum", [P, NJ])
        a_neg = sb("a_neg", [P, NJ])
        d_sb = sb("d_sb", [INNER, 1])
        wy_in = sb("wy_in", [P, D])
        wy_neg = sb("wy_neg", [P, D])
        wyz_in = sb("wyz_in", [P, D])
        wxz = sb("wxz", [P, D])
        power = sb("power", [P, TILES])
        quarter = sb("quarter", [P, TILES])

        x_sb = [sb(f"x_sb{s}", [P, TILES, D]) for s in range(2)]
        xt_hi = [sb(f"xt_hi{s}", [P, GROUP], F32R) for s in range(2)]
        xt_lo = [sb(f"xt_lo{s}", [P, GROUP], F32R) for s in range(2)]
        gates = [sb(f"gates{s}", [P, TILES, EXPERTS]) for s in range(2)]
        h_in = [sb(f"h_in{s}", [P, GROUP + 2]) for s in range(2)]
        acc = [sb(f"acc{s}", [P, TILES, D]) for s in range(2)]

        bn = sb("bn", [P, TILES, 6])
        mean_sum = sb("mean_sum", [P, TILES])
        mean_gap = sb("mean_gap", [P, TILES])
        gap_sq = sb("gap_sq", [P, TILES])
        square_sum = sb("square_sum", [P, TILES])
        mean = sb("mean", [P, TILES])
        var_eps = sb("var_eps", [P, TILES])
        rstd = sb("rstd", [P, TILES])
        xn = sb("xn", [P, TILES, D])
        score = sb("score", [P, TILES, EXPERTS])
        score2 = sb("score2", [P, TILES, EXPERTS])
        top = [sb(f"top{n}", [P, TILES]) for n in range(2)]
        hit = [sb(f"hit{n}", [P, TILES, EXPERTS]) for n in range(2)]
        keyed = [sb(f"keyed{n}", [P, TILES, EXPERTS]) for n in range(2)]
        key_max = [sb(f"key_max{n}", [P, TILES]) for n in range(2)]
        one_hot = [sb(f"one_hot{n}", [P, TILES, EXPERTS]) for n in range(2)]
        margin = sb("margin", [P, TILES])
        lean = sb("lean", [P, TILES])
        both = sb("both", [P, TILES, EXPERTS])
        apart = sb("apart", [P, TILES, EXPERTS])
        leaned = sb("leaned", [P, TILES, EXPERTS])

        g_sb = [sb(f"g_sb{a}", [P, GROUP]) for a in range(2)]
        hid = [[sb(f"hid{s}{a}", [P, GROUP]) for a in range(HALVES)] for s in range(2)]
        gated = [sb(f"gated{s}", [P, TILES, D]) for s in range(2)]

        conv = sb("conv", [P, GROUP])
        xz = sb("xz", [P, GROUP])
        xx = sb("xx", [P, GROUP])
        bc = sb("bc", [P, GROUP])
        bc_r = sb("bc_r", [P, GROUP], F32R)
        pre = sb("pre", [INNER, GROUP])
        pre_exp = sb("pre_exp", [INNER, GROUP])
        delta = sb("delta", [P, GROUP])
        decay = [sb(f"decay{j}", [P, GROUP]) for j in range(NJ)]
        bx = [sb(f"bx{j}", [P, GROUP]) for j in range(NJ)]
        state = [[sb(f"state{s}{j}", [P, GROUP]) for j in range(NJ)] for s in range(2)]
        mix = sb("mix", [P, TILES, D])

        h_ps = [ctx.enter_context(nc.psum_tensor(f"h_ps{a}", [P, 2, GROUP], F32)) for a in range(2)]
        y_ps = [ctx.enter_context(nc.psum_tensor(f"y_ps{s}", [P, TILES, D], F32)) for s in range(2)]
        s_ps = [ctx.enter_context(nc.psum_tensor(f"s_ps{s}", [P, GROUP], F32)) for s in range(2)]

        small_loaded = event("small_loaded")
        late_loaded = event("late_loaded")
        w12_loaded = [event(f"w12_loaded{e}") for e in range(EXPERTS)]
        w3_loaded = event("w3_loaded")
        x_loaded = [event(f"x_loaded{s}") for s in range(2)]
        consts_set = event("consts_set")
        win_hi_done = event("win_hi_done")
        win_lo_done = event("win_lo_done")
        w12_hi_done = event("w12_hi_done")
        w12_lo_done = event("w12_lo_done")
        a_dve_step = event("a_dve_step")
        a_act_step = event("a_act_step")
        sel_done = event("sel_done")
        w_comb_full = event("w_comb_full")
        wp_done = event("wp_done")
        w_out_done = event("w_out_done")
        bn_done = stage("bn_done", TILES, TILES)
        rstd_step = stage("rstd_step", RSTD_STEPS, RSTD_STEPS)
        xn_done = stage("xn_done", TILES, TILES)
        xt_full = stage("xt_full", 1, 1)
        xt_hi_done = stage("xt_hi_done", 1, 1)
        xt_lo_done = stage("xt_lo_done", 1, 1)
        score_full = stage("score_full", 1, 1)
        h_in_full = stage("h_in_full", 1, 1)
        h_in_done = stage("h_in_done", 1, 1)
        gate_stepped = stage("gate_stepped", GATE_STEPS, GATE_STEPS)
        lean_done = stage("lean_done", 1, 1)
        h_full = stage("h_full", UNITS * HALVES)
        silu_done = stage("silu_done", UNITS * HALVES)
        hid_done = stage("hid_done", UNITS * HALVES, 2)
        y_full = stage("y_full", UNITS, 2)
        gated_done = stage("gated_done", UNITS, 2)
        acc_done = stage("acc_done", UNITS + 1, 2)
        out_stored = [event(f"out_stored{s}") for s in range(2)]
        conv_stepped = stage("conv_stepped", 3)
        xz_done = stage("xz_done", 3)
        proj_full = stage("proj_full", 1)
        bc_tanh_done = stage("bc_tanh_done", 1)
        pre_done = stage("pre_done", 1)
        bc_split = stage("bc_split", 2)
        bc_full = stage("bc_full", 2 * NJ)
        softplus_step = stage("softplus_step", 3)
        delta_done = stage("delta_done", 1)
        decay_done = stage("decay_done", NJ)
        clip_done = stage("clip_done", NJ)
        bx_done = stage("bx_done", NJ)
        drive_done = stage("drive_done", NJ)
        scan_done = stage("scan_done", NJ)
        c_state_done = stage("c_state_done", NJ)
        state_sum_step = stage("state_sum_step", NJ - 1)
        mix_full = stage("mix_full", 1)
        mix_done = stage("mix_done", 1, 1)

        block = ctx.enter_context(nc.Block())

        USES = ["xt", "score", "h_in", "proj"] + [f"bc{n}" for n in range(2 * NJ)] + ["mix"]

        def bank(g, use):
            return s_ps[(g * len(USES) + USES.index(use)) % 2]

        comb_ps = bank(-1, "proj")

        def flat(t):
            return t[:, :, :].rearrange("p t d -> p (t d)")

        SMALL = ((id_sb, ident), (win_f, w_in_t), (gate_f, gate_t), (key_sb, rank_key))
        LATE = ((sel_f, select), (taps, conv_taps), (wx_dt_sb, wx_dt), (w_dt_sb, w_dt_t), (b_dt_sb, b_dt),
                (a_in, a_log), (d_sb, d_skip), (wy_in, w_out_y), (wyz_in, w_out_yz), (wx_bc_sb, wx_bc_t))

        @block.sync
        def _(sp):
            sp.dma_start(x_sb[0][:, :, :], x_v[0, 0]).then_inc(x_loaded[0], 16)
            for dst, src in SMALL:
                sp.dma_start(dst[:], src).then_inc(small_loaded, 16)
            sp.dma_start(w12_f[:, 0, :], w12_t[:, 0, :]).then_inc(w12_loaded[0], 16)
            for dst, src in LATE:
                sp.dma_start(dst[:], src).then_inc(late_loaded, 16)
            for e in range(1, EXPERTS):
                sp.dma_start(w12_f[:, e, :], w12_t[:, e, :]).then_inc(w12_loaded[e], 16)
            sp.dma_start(x_sb[1][:, :, :], x_v[0, 1]).then_inc(x_loaded[1], 16)
            sp.dma_start(w3_sb[:, :, :, :], w3_t).then_inc(w3_loaded, 16)
            with sp.Fori(0, BATCHES) as i:
                for g in range(GROUPS):
                    w = i * GROUPS + g
                    sp.wait_ge(acc_done.sem, acc_done.at(w, 1))
                    sp.dma_start(x_sb[g][:, :, :], x_v[(i + 1) % BATCHES, g]).then_inc(x_loaded[g], 16)
                    sp.wait_ge(acc_done.sem, acc_done.at(w, UNITS + 1))
                    sp.dma_start(out_v[i, g], acc[g][:, :, :]).then_inc(out_stored[g], 16)
            for g in range(GROUPS):
                sp.wait_ge(out_stored[g], 16 * (BATCHES + 1))
                sp.wait_ge(x_loaded[g], 16 * (BATCHES + 1))

        @block.gpsimd
        def _(pool):
            for st in (hid_done, y_full, gated_done, acc_done, mix_done):
                pool.sem_inc(st.sem, st.base)
            for s in range(2):
                pool.sem_inc(out_stored[s], 16)
            nc.gpsimd.memset(wp[:, :], 0.0).then_inc(consts_set, 1)
            nc.gpsimd.memset(power[:, :], -0.5).then_inc(consts_set, 1)
            nc.gpsimd.memset(quarter[:, :], 0.25).then_inc(consts_set, 1)
            nc.gpsimd.memset(h_in[0][:, 0:1], 0.0).then_inc(consts_set, 1)
            nc.gpsimd.memset(h_in[1][:, GROUP + 1:GROUP + 2], 0.0).then_inc(consts_set, 1)
            pool.wait_ge(consts_set, 5)

            def inverse_deviation(w):
                even, odd = bn[:, :, 0:3], bn[:, :, 3:6]
                pool.wait_ge(bn_done.sem, bn_done.at(w, TILES))
                nc.gpsimd.tensor_tensor(mean_sum[:, :], even[:, :, 1], odd[:, :, 1], ALU.add)
                nc.gpsimd.tensor_tensor(mean_gap[:, :], even[:, :, 1], odd[:, :, 1], ALU.subtract)
                nc.gpsimd.tensor_tensor(square_sum[:, :], even[:, :, 2], odd[:, :, 2], ALU.add).then_inc(rstd_step.sem, 1)
                pool.wait_ge(rstd_step.sem, rstd_step.at(w, 1))
                nc.gpsimd.tensor_tensor(gap_sq[:, :], mean_gap[:, :], mean_gap[:, :], ALU.mult)
                nc.gpsimd.tensor_scalar(mean[:, :], mean_sum[:, :], 0.5, 0.0, ALU.mult, ALU.add)
                nc.gpsimd.tensor_scalar(square_sum[:, :], square_sum[:, :], 1.0 / D, LN_EPS, ALU.mult, ALU.add).then_inc(rstd_step.sem, 1)
                pool.wait_ge(rstd_step.sem, rstd_step.at(w, 2))
                nc.gpsimd.tensor_tensor(gap_sq[:, :], gap_sq[:, :], quarter[:, :], ALU.mult).then_inc(rstd_step.sem, 1)
                pool.wait_ge(rstd_step.sem, rstd_step.at(w, 3))
                nc.gpsimd.tensor_tensor(var_eps[:, :], square_sum[:, :], gap_sq[:, :], ALU.add).then_inc(rstd_step.sem, 1)
                pool.wait_ge(rstd_step.sem, rstd_step.at(w, 4))
                nc.gpsimd.tensor_tensor(rstd[:, :], var_eps[:, :], power[:, :], ALU.pow).then_inc(rstd_step.sem, 1)

            inverse_deviation(-1)
            with pool.Fori(0, BATCHES) as i:
                for g in range(GROUPS):
                    w = i * GROUPS + g

                    def add_expert(u):
                        pool.wait_ge(gated_done.sem, gated_done.at(w, u + 1))
                        if u == 0:
                            pool.wait_ge(out_stored[g], i * 16 + 16)
                        else:
                            pool.wait_ge(acc_done.sem, acc_done.at(w, u))
                        nc.gpsimd.tensor_tensor(flat(acc[g]), flat(acc[g] if u else x_sb[g]), flat(gated[u % 2]),
                                                ALU.add).then_inc(acc_done.sem, 1)

                    def sum_pair(p):
                        pool.wait_ge(c_state_done.sem, c_state_done.at(w, 2 * p + 2))
                        nc.gpsimd.tensor_tensor(bx[2 * p][:, :], bx[2 * p][:, :], bx[2 * p + 1][:, :],
                                                ALU.add).then_inc(state_sum_step.sem, 1)

                    inverse_deviation(w)
                    for u in range(UNITS):
                        add_expert(u)
                        if u == 5:
                            sum_pair(0)
                        if u == 6:
                            sum_pair(1)
                            pool.wait_ge(state_sum_step.sem, state_sum_step.at(w, 2))
                            nc.gpsimd.tensor_tensor(bx[0][:, :], bx[0][:, :], bx[2][:, :], ALU.add).then_inc(state_sum_step.sem, 1)
                    pool.wait_ge(mix_done.sem, mix_done.at(w, 1))
                    pool.wait_ge(acc_done.sem, acc_done.at(w, UNITS))
                    nc.gpsimd.tensor_tensor(flat(acc[g]), flat(acc[g]), flat(mix), ALU.add).then_inc(acc_done.sem, 1)

        @block.scalar
        def _(act):
            def keep_xt_hi(w, slot, ps):
                act.wait_ge(xt_full.sem, xt_full.at(w, 1))
                nc.scalar.copy(xt_hi[slot][:, :], ps[:, :]).then_inc(xt_hi_done.sem, 1)

            def keep_h_in(w, slot, ps, halo):
                act.wait_ge(h_in_full.sem, h_in_full.at(w, 1))
                last = nc.scalar.copy(h_in[slot][:, 1:GROUP + 1], ps[:, :])
                if halo:
                    nc.scalar.copy(h_in[0][:, GROUP + 1:GROUP + 2], ps[:, 0:1])
                    last = nc.scalar.copy(h_in[1][:, 0:1], h_in[0][:, GROUP:GROUP + 1])
                last.then_inc(h_in_done.sem, 1)

            def lean_to_best(w):
                act.wait_ge(gate_stepped.sem, gate_stepped.at(w, MARGIN_STEP + 1))
                nc.scalar.activation(lean[:, :], margin[:, :], ACT.Tanh, scale=0.5).then_inc(lean_done.sem, 1)

            keep_xt_hi(-1, 0, bank(-1, "xt"))
            act.wait_ge(small_loaded, 16 * len(SMALL))
            nc.scalar.copy(win_hi[:, :], win_f[:, :])
            nc.scalar.copy(gate_hi[:, :], gate_f[:, :]).then_inc(win_hi_done, 1)
            act.wait_ge(w12_loaded[0], 16)
            nc.scalar.copy(w12_hi[:, 0, :], w12_f[:, 0, :]).then_inc(w12_hi_done, 1)
            keep_h_in(-1, 0, bank(-1, "h_in"), False)
            act.wait_ge(late_loaded, 16 * len(LATE))
            nc.scalar.copy(sel_r[INNER:P, :, :], sel_f[INNER:P, :, :]).then_inc(sel_done, 1)
            act.wait_ge(consts_set, 1)
            for at in (INNER, INNER + 32):
                nc.scalar.copy(wp[:, at:at + 2 * DSTATE], wx_bc_sb[:, :])
            act.wait_ge(w_comb_full, 1)
            nc.scalar.copy(wp[:, 0:INNER], comb_ps[0:INNER, 0:INNER]).then_inc(wp_done, 1)
            nc.scalar.preload_act_table_set("natural_log_exp_and_others")
            act.wait_ge(a_dve_step, 1)
            nc.scalar.activation(a_exp[:, :], a_abs[:, :], ACT.Exp, scale=-1.0).then_inc(a_act_step, 1)
            act.wait_ge(a_act_step, 1)
            nc.scalar.activation(a_ln[:, :], a_exp[:, :], ACT.Ln, bias=1.0).then_inc(a_act_step, 1)
            nc.scalar.preload_act_table_set("silu_and_others")
            for e in range(1, EXPERTS):
                act.wait_ge(w12_loaded[e], 16)
                nc.scalar.copy(w12_hi[:, e, :], w12_f[:, e, :]).then_inc(w12_hi_done, 1)
            lean_to_best(-1)

            with act.Fori(0, BATCHES) as i:
                for g in range(GROUPS):
                    w = i * GROUPS + g

                    def silu(u, a):
                        act.wait_ge(h_full.sem, h_full.at(w, HALVES * u + a + 1))
                        nc.scalar.activation(g_sb[a][:, :], h_ps[a][:, 0, :], ACT.Silu).then_inc(silu_done.sem, 1)

                    def conv_silu():
                        act.wait_ge(conv_stepped.sem, conv_stepped.at(w, 3))
                        nc.scalar.activation(xz[:, :], conv[:, :], ACT.Silu).then_inc(xz_done.sem, 1)
                        nc.scalar.activation(xx[0:INNER, :], conv[0:INNER, :], ACT.Silu).then_inc(xz_done.sem, 1)
                        nc.scalar.activation(xx[INNER:P, :], conv[0:INNER, :], ACT.Silu).then_inc(xz_done.sem, 1)

                    def bc_tanh():
                        act.wait_ge(proj_full.sem, proj_full.at(w, 1))
                        nc.scalar.activation(bc[INNER:P, :], bank(g, "proj")[INNER:P, :], ACT.Tanh).then_inc(bc_tanh_done.sem, 1)

                    def softplus():
                        act.wait_ge(pre_done.sem, pre_done.at(w, 1))
                        nc.scalar.activation(pre_exp[:, :], pre[:, :], ACT.Exp).then_inc(softplus_step.sem, 1)
                        act.wait_ge(softplus_step.sem, softplus_step.at(w, 1))
                        nc.scalar.activation(delta[0:INNER, :], pre_exp[:, :], ACT.Ln, bias=1.0).then_inc(softplus_step.sem, 1)
                        nc.scalar.activation(delta[INNER:P, :], pre_exp[:, :], ACT.Ln, bias=1.0).then_inc(softplus_step.sem, 1)

                    def decay_exp():
                        act.wait_ge(delta_done.sem, delta_done.at(w, 1))
                        for j in range(NJ):
                            nc.scalar.activation(decay[j][:, :], delta[:, :], ACT.Exp, scale=a_neg[:, j:j + 1]).then_inc(decay_done.sem, 1)

                    for u in range(UNITS):
                        silu(u, 0)
                        if u == 1:
                            keep_xt_hi(w, 1 - g, bank(g, "xt"))
                        silu(u, 1)
                        if u == 1:
                            keep_h_in(w, 1 - g, bank(g, "h_in"), g == 0)
                        if u == 2:
                            conv_silu()
                        if u == 3:
                            bc_tanh()
                            nc.scalar.preload_act_table_set("natural_log_exp_and_others")
                            softplus()
                            decay_exp()
                            nc.scalar.preload_act_table_set("silu_and_others")
                        if u == 6:
                            lean_to_best(w)

        @block.vector
        def _(dve):
            def statistics(w, slot, loads):
                dve.wait_ge(x_loaded[slot], loads * 16)
                for t in range(TILES):
                    nc.vector.bn_stats(bn[:, t, :], x_sb[slot][:, t, :]).then_inc(bn_done.sem, 1)

            def normalise(w, slot):
                dve.wait_ge(rstd_step.sem, rstd_step.at(w, RSTD_STEPS))
                for t in range(TILES):
                    nc.vector.tensor_scalar(xn[:, t, :], x_sb[slot][:, t, :], mean[:, t:t + 1], rstd[:, t:t + 1],
                                            ALU.subtract, ALU.mult).then_inc(xn_done.sem, 1)

            def keep_xt_lo(w, slot, ps):
                dve.wait_ge(xt_hi_done.sem, xt_hi_done.at(w, 1))
                nc.vector.tensor_tensor(xt_lo[slot][:, :], ps[:, :], xt_hi[slot][:, :].bitcast(F32), ALU.subtract).then_inc(xt_lo_done.sem, 1)

            def wide(t):
                return t[:, :].unsqueeze(2).to_broadcast([P, TILES, EXPERTS])

            def gate_step(w, slot, ps, n):
                if n == 0:
                    dve.wait_ge(score_full.sem, score_full.at(w, 1))
                    last = nc.vector.tensor_copy(flat(score), ps[:, 0:TILES * EXPERTS])
                else:
                    dve.wait_ge(gate_stepped.sem, gate_stepped.at(w, n))
                k, from_, m = (0, score, n - 1) if n < 6 else (1, score2, n - 7 if n < 9 else n - 8)
                if n == 6:
                    last = nc.vector.scalar_tensor_tensor(out=score2[:, :, :], in0=one_hot[0][:, :, :], scalar=LOWEST,
                                                          in1=score[:, :, :], op0=ALU.mult, op1=ALU.add)
                elif n == MARGIN_STEP:
                    last = nc.vector.tensor_tensor(margin[:, :], top[0][:, :], top[1][:, :], ALU.subtract)
                elif n == 13:
                    nc.vector.tensor_tensor(both[:, :, :], one_hot[0][:, :, :], one_hot[1][:, :, :], ALU.add)
                    last = nc.vector.tensor_tensor(apart[:, :, :], one_hot[0][:, :, :], one_hot[1][:, :, :], ALU.subtract)
                elif n == 14:
                    dve.wait_ge(lean_done.sem, lean_done.at(w, 1))
                    last = nc.vector.scalar_tensor_tensor(out=leaned[:, :, :], in0=apart[:, :, :], scalar=0.5,
                                                          in1=wide(lean), op0=ALU.mult, op1=ALU.mult)
                elif n == 15:
                    last = nc.vector.scalar_tensor_tensor(out=gates[slot][:, :, :], in0=both[:, :, :], scalar=0.5,
                                                          in1=leaned[:, :, :], op0=ALU.mult, op1=ALU.add)
                elif n > 0 and m == 0:
                    last = nc.vector.tensor_reduce(top[k][:, :], from_[:, :, :], AX_X, ALU.max)
                elif n > 0 and m == 1:
                    last = nc.vector.tensor_tensor(hit[k][:, :, :], from_[:, :, :], wide(top[k]), ALU.is_equal)
                elif n > 0 and m == 2:
                    last = nc.vector.tensor_tensor(keyed[k][:, :, :], hit[k][:, :, :], key_sb[:, :, :], ALU.mult)
                elif n > 0 and m == 3:
                    last = nc.vector.tensor_reduce(key_max[k][:, :], keyed[k][:, :, :], AX_X, ALU.max)
                elif n > 0 and m == 4:
                    last = nc.vector.tensor_tensor(one_hot[k][:, :, :], keyed[k][:, :, :], wide(key_max[k]), ALU.is_equal)
                last.then_inc(gate_stepped.sem, 1)

            statistics(-1, 0, 1)
            normalise(-1, 0)
            keep_xt_lo(-1, 0, bank(-1, "xt"))
            dve.wait_ge(win_hi_done, 1)
            nc.vector.tensor_tensor(win_lo[:, :], win_f[:, :], win_hi[:, :].bitcast(F32), ALU.subtract)
            nc.vector.tensor_tensor(gate_lo[:, :], gate_f[:, :], gate_hi[:, :].bitcast(F32), ALU.subtract).then_inc(win_lo_done, 1)
            dve.wait_ge(w12_hi_done, 1)
            nc.vector.tensor_tensor(w12_lo[:, 0, :], w12_f[:, 0, :], w12_hi[:, 0, :].bitcast(F32), ALU.subtract).then_inc(w12_lo_done, 1)
            gate_step(-1, 0, bank(-1, "score"), 0)
            dve.wait_ge(late_loaded, 16 * len(LATE))
            nc.vector.scalar_tensor_tensor(out=a_abs[:, :], in0=a_in[:, :], scalar=-1.0, in1=a_in[:, :],
                                           op0=ALU.mult, op1=ALU.max).then_inc(a_dve_step, 1)
            nc.vector.tensor_scalar(wy_neg[:, :], wy_in[:, :], -1.0, None, ALU.mult).then_inc(w_out_done, 1)
            nc.vector.tensor_scalar(wxz[0:INNER, :], wyz_in[0:INNER, :], d_sb[:, 0:1], None, ALU.mult).then_inc(w_out_done, 1)
            nc.vector.tensor_copy(wxz[INNER:P, :], wyz_in[INNER:P, :]).then_inc(w_out_done, 1)
            dve.wait_ge(a_act_step, 2)
            nc.vector.scalar_tensor_tensor(out=a_sum[:, :], in0=a_in[:, :], scalar=0.0, in1=a_ln[:, :],
                                           op0=ALU.max, op1=ALU.add).then_inc(a_dve_step, 1)
            dve.wait_ge(a_dve_step, 2)
            nc.vector.tensor_scalar(a_neg[:, :], a_sum[:, :], A_MIN, -1.0, ALU.add, ALU.mult).then_inc(a_dve_step, 1)
            for e in range(1, EXPERTS):
                dve.wait_ge(w12_hi_done, e + 1)
                nc.vector.tensor_tensor(w12_lo[:, e, :], w12_f[:, e, :], w12_hi[:, e, :].bitcast(F32), ALU.subtract).then_inc(w12_lo_done, 1)
                for n in range(2 * e - 1, 2 * e + 1):
                    gate_step(-1, 0, bank(-1, "score"), n)
            for n in range(2 * EXPERTS - 1, GATE_STEPS):
                gate_step(-1, 0, bank(-1, "score"), n)

            with dve.Fori(0, BATCHES) as i:
                for g in range(GROUPS):
                    w = i * GROUPS + g

                    def product(u, a):
                        dve.wait_ge(silu_done.sem, silu_done.at(w, HALVES * u + a + 1))
                        dve.wait_ge(y_full.sem, y_full.at(w, u - 1))
                        nc.vector.tensor_tensor(hid[u % 2][a][:, :], h_ps[a][:, 1, :], g_sb[a][:, :], ALU.mult).then_inc(hid_done.sem, 1)

                    def gate(u):
                        dve.wait_ge(y_full.sem, y_full.at(w, u + 1))
                        dve.wait_ge(acc_done.sem, acc_done.at(w, u - 1 if u > 1 else u - 2))
                        if u == 0:
                            dve.wait_ge(gate_stepped.sem, gate_stepped.at(w - 1, GATE_STEPS))
                        nc.vector.tensor_tensor(gated[u % 2][:, :, :], y_ps[u % 2][:, :, :],
                                                gates[g][:, :, u].unsqueeze(2).to_broadcast([P, TILES, D]), ALU.mult).then_inc(gated_done.sem, 1)

                    def convolve():
                        dve.wait_ge(h_in_done.sem, h_in_done.at(w, 1))
                        nc.vector.tensor_scalar(conv[:, :], h_in[g][:, 0:GROUP], taps[:, 0:1], None, ALU.mult).then_inc(conv_stepped.sem, 1)
                        for k in range(1, 3):
                            dve.wait_ge(conv_stepped.sem, conv_stepped.at(w, k))
                            nc.vector.scalar_tensor_tensor(out=conv[:, :], in0=h_in[g][:, k:k + GROUP], scalar=taps[:, k:k + 1],
                                                           in1=conv[:, :], op0=ALU.mult, op1=ALU.add).then_inc(conv_stepped.sem, 1)

                    def keep_pre():
                        dve.wait_ge(proj_full.sem, proj_full.at(w, 1))
                        nc.vector.tensor_scalar(pre[:, :], bank(g, "proj")[0:INNER, :], b_dt_sb[:, 0:1], PRE_MAX,
                                                ALU.add, ALU.min).then_inc(pre_done.sem, 1)

                    def split_bc():
                        dve.wait_ge(bc_tanh_done.sem, bc_tanh_done.at(w, 1))
                        nc.vector.tensor_copy(bc_r[INNER:P, :], bc[INNER:P, :]).then_inc(bc_split.sem, 1)
                        dve.wait_ge(bc_split.sem, bc_split.at(w, 1))
                        nc.vector.tensor_tensor(bc_r[INNER + 32:P, :], bc[INNER + 32:P, :], bc_r[INNER + 32:P, :].bitcast(F32),
                                                ALU.subtract).then_inc(bc_split.sem, 1)

                    def b_times_x(j):
                        dve.wait_ge(bc_full.sem, bc_full.at(w, j + 1))
                        if j == 0:
                            dve.wait_ge(xz_done.sem, xz_done.at(w, 3))
                        nc.vector.tensor_tensor(bx[j][:, :], bank(g, f"bc{j}")[:, :], xx[:, :], ALU.mult).then_inc(bx_done.sem, 1)

                    def clip_delta():
                        dve.wait_ge(softplus_step.sem, softplus_step.at(w, 3))
                        nc.vector.tensor_scalar(delta[:, :], delta[:, :], CLIP_MIN, 1.0, ALU.max, ALU.min).then_inc(delta_done.sem, 1)

                    def clip_decay(j):
                        dve.wait_ge(decay_done.sem, decay_done.at(w, j + 1))
                        nc.vector.tensor_scalar(decay[j][:, :], decay[j][:, :], CLIP_MIN, 1.0, ALU.max, ALU.min).then_inc(clip_done.sem, 1)

                    def negative_drive(j):
                        dve.wait_ge(clip_done.sem, clip_done.at(w, j + 1))
                        dve.wait_ge(bx_done.sem, bx_done.at(w, j + 1))
                        nc.vector.scalar_tensor_tensor(out=bx[j][:, :], in0=decay[j][:, :], scalar=1.0, in1=bx[j][:, :],
                                                       op0=ALU.subtract, op1=ALU.mult).then_inc(drive_done.sem, 1)

                    def scan(j):
                        dve.wait_ge(drive_done.sem, drive_done.at(w, j + 1))
                        first = 0.0 if g == 0 else state[0][j][:, GROUP - 1:GROUP]
                        nc.vector.tensor_tensor_scan(state[g][j][:, :], decay[j][:, :], bx[j][:, :], first, ALU.mult, ALU.add).then_inc(scan_done.sem, 1)

                    def c_times_state(j):
                        dve.wait_ge(bc_full.sem, bc_full.at(w, NJ + j + 1))
                        dve.wait_ge(scan_done.sem, scan_done.at(w, j + 1))
                        nc.vector.tensor_tensor(bx[j][:, :], bank(g, f"bc{NJ + j}")[:, :], state[g][j][:, :], ALU.mult).then_inc(c_state_done.sem, 1)

                    def keep_mix():
                        dve.wait_ge(mix_full.sem, mix_full.at(w, 1))
                        nc.vector.tensor_copy(flat(mix), bank(g, "mix")[:, :]).then_inc(mix_done.sem, 1)

                    def next_gate(first, end):
                        for n in range(first, end):
                            gate_step(w, 1 - g, bank(g, "score"), n)

                    statistics(w, 1 - g, i + 1 + g)
                    for u in range(UNITS):
                        product(u, 0)
                        if u == 5:
                            negative_drive(0)
                            b_times_x(2)
                            scan(0)
                        if u == 6:
                            c_times_state(0)
                            scan(2)
                        if u == 7:
                            c_times_state(2)
                        product(u, 1)
                        if u > 0:
                            gate(u - 1)
                        if u == 0:
                            normalise(w, 1 - g)
                        if u == 1:
                            keep_xt_lo(w, 1 - g, bank(g, "xt"))
                            next_gate(0, 1)
                        if u == 2:
                            convolve()
                        if u == 3:
                            keep_pre()
                            next_gate(1, 4)
                            clip_delta()
                            split_bc()
                        if u == 4:
                            b_times_x(0)
                            clip_decay(0)
                            b_times_x(1)
                            clip_decay(1)
                            next_gate(4, 8)
                        if u == 5:
                            negative_drive(1)
                            b_times_x(3)
                            scan(1)
                            clip_decay(2)
                            clip_decay(3)
                            negative_drive(2)
                            next_gate(8, 12)
                        if u == 6:
                            c_times_state(1)
                            negative_drive(3)
                            scan(3)
                        if u == 7:
                            c_times_state(3)
                            next_gate(12, GATE_STEPS)
                            keep_mix()
                    gate(UNITS - 1)

        @block.tensor
        def _(pe):
            def transpose_xn(w, ps):
                pe.wait_ge(xn_done.sem, xn_done.at(w, TILES))
                for t in range(TILES):
                    last = nc.tensor.transpose(ps[:, t * P:(t + 1) * P], xn[:, t, :], id_sb[:, :])
                last.then_inc(xt_full.sem, 1)

            def three_pass(out_ps, left_hi, left_lo, right_hi, right_lo):
                nc.tensor.matmul(out_ps, left_lo, right_hi, start=True, stop=False)
                nc.tensor.matmul(out_ps, left_hi, right_lo, start=False, stop=False)
                return nc.tensor.matmul(out_ps, left_hi, right_hi, start=False, stop=True)

            def scores(w, slot, ps):
                pe.wait_ge(xt_lo_done.sem, xt_lo_done.at(w, 1))
                for t in range(TILES):
                    c = slice(t * P, (t + 1) * P)
                    last = three_pass(ps[:, t * EXPERTS:(t + 1) * EXPERTS], xt_hi[slot][:, c], xt_lo[slot][:, c],
                                      gate_hi[:, :], gate_lo[:, :])
                last.then_inc(score_full.sem, 1)

            def project_in(w, slot, ps):
                three_pass(ps[:, :], win_hi[:, :], win_lo[:, :], xt_hi[slot][:, :], xt_lo[slot][:, :]).then_inc(h_in_full.sem, 1)

            pe.wait_ge(small_loaded, 16 * len(SMALL))
            transpose_xn(-1, bank(-1, "xt"))
            pe.wait_ge(win_lo_done, 1)
            scores(-1, 0, bank(-1, "score"))
            project_in(-1, 0, bank(-1, "h_in"))
            pe.wait_ge(gate_stepped.sem, 1)
            pe.wait_ge(late_loaded, 16 * len(LATE))
            nc.tensor.matmul(comb_ps[0:INNER, 0:INNER], wx_dt_sb[:, :], w_dt_sb[:, :], start=True, stop=True).then_inc(w_comb_full, 1)
            pe.wait_ge(wp_done, 1)
            pe.wait_ge(h_in_done.sem, h_in_done.at(-1, 1))
            pe.wait_ge(sel_done, 1)
            pe.wait_ge(w_out_done, 3)

            with pe.Fori(0, BATCHES) as i:
                for g in range(GROUPS):
                    w = i * GROUPS + g

                    def hidden(u, a):
                        if g == 0 and a == 0:
                            pe.wait_ge(w12_lo_done, u + 1)
                        pe.wait_ge(hid_done.sem, hid_done.at(w, HALVES * u + a - 1))
                        for part in range(2):
                            c = slice((part * HALVES + a) * P, (part * HALVES + a + 1) * P)
                            last = three_pass(h_ps[a][:, part, :], w12_hi[:, u, c], w12_lo[:, u, c], xt_hi[g][:, :], xt_lo[g][:, :])
                        last.then_inc(h_full.sem, 1)

                    def expert_out(u):
                        if g == 0 and u == 0:
                            pe.wait_ge(w3_loaded, 16)
                        pe.wait_ge(hid_done.sem, hid_done.at(w, HALVES * (u + 1)))
                        pe.wait_ge(gated_done.sem, gated_done.at(w, u - 1))
                        for t in range(TILES):
                            for a in range(HALVES):
                                last = nc.tensor.matmul(y_ps[u % 2][:, t, :], hid[u % 2][a][:, t * P:(t + 1) * P], w3_sb[:, u, a, :],
                                                        start=(a == 0), stop=(a == HALVES - 1))
                        last.then_inc(y_full.sem, 1)

                    def project():
                        pe.wait_ge(xt_lo_done.sem, xt_lo_done.at(w, 1))
                        pe.wait_ge(gate_stepped.sem, gate_stepped.at(w, 1))
                        pe.wait_ge(xz_done.sem, xz_done.at(w, 1))
                        nc.tensor.matmul(bank(g, "proj")[:, :], wp[:, :], xz[0:INNER, :], start=True, stop=True).then_inc(proj_full.sem, 1)

                    def spread(n):
                        if n == 0:
                            pe.wait_ge(bc_split.sem, bc_split.at(w, 2))
                            pe.wait_ge(h_in_done.sem, h_in_done.at(w, 1))
                        elif n == 1:
                            pe.wait_ge(pre_done.sem, pre_done.at(w, 1))
                            pe.wait_ge(bc_tanh_done.sem, bc_tanh_done.at(w, 1))
                        elif n < NJ + 2:
                            pe.wait_ge(bx_done.sem, bx_done.at(w, n - 1))
                        else:
                            pe.wait_ge(c_state_done.sem, c_state_done.at(w, n - NJ - 1))
                        nc.tensor.matmul(bank(g, f"bc{n}")[:, :], sel_r[INNER:P, n, :], bc_r[INNER:P, :], start=True, stop=True).then_inc(bc_full.sem, 1)

                    def project_out():
                        pe.wait_ge(state_sum_step.sem, state_sum_step.at(w, 3))
                        for t in range(TILES):
                            c = slice(t * P, (t + 1) * P)
                            nc.tensor.matmul(bank(g, "mix")[:, c], bx[0][:, c], wy_neg[:, :], start=True, stop=False)
                            last = nc.tensor.matmul(bank(g, "mix")[:, c], xz[:, c], wxz[:, :], start=False, stop=True)
                        last.then_inc(mix_full.sem, 1)

                    for u in range(UNITS):
                        hidden(u, 0)
                        if u == 1:
                            transpose_xn(w, bank(g, "xt"))
                        if u == 5:
                            spread(2)
                        if u == 6:
                            spread(4)
                        if u == 7:
                            spread(6)
                        hidden(u, 1)
                        if u > 0:
                            expert_out(u - 1)
                        if u == 1:
                            pe.wait_ge(mix_done.sem, mix_done.at(w - 1, 1))
                            scores(w, 1 - g, bank(g, "score"))
                            project_in(w, 1 - g, bank(g, "h_in"))
                        if u == 3:
                            project()
                        if u == 4:
                            spread(0)
                            spread(1)
                        if u == 5:
                            spread(3)
                        if u == 6:
                            spread(5)
                        if u == 7:
                            spread(7)
                            project_out()
                    expert_out(UNITS - 1)


def kernel(**inputs):
    import numpy as np
    import concourse.bacc as bacc
    from concourse.bass_utils import run_bass_kernel_spmd

    def arr(name):
        return np.asarray(inputs[name])

    w_xproj = arr("L0_attn_W_xproj")
    w_dt = arr("L0_attn_W_dt")
    inner, dtr = w_dt.shape
    dstate = (w_xproj.shape[0] - dtr) // 2
    w_out_t = arr("L0_attn_W_out").T
    w12, w3, gate_w = arr("L0_ffn_w12"), arr("L0_ffn_w3"), arr("L0_ffn_gate_w")
    experts, d, hidden = w3.shape
    nj = dstate * inner // P
    a_log = arr("L0_attn_A_log").T.reshape(nj, P).T
    taps = np.concatenate([arr("L0_attn_Kx")[:, 0, :], arr("L0_attn_Kz")[:, 0, :]], axis=0)
    select = np.zeros((P, 2 * nj, P), np.float32)
    for n in range(2 * nj):
        for member in range(2):
            row = (n // nj) * dstate + 2 * (n % nj) + member
            for copy in (inner, inner + 32):
                select[copy + row, n, member * inner:(member + 1) * inner] = 1.0
    rank_key = np.broadcast_to(np.arange(experts, 0, -1, dtype=np.float32), (P, TILES, experts))
    arrays = {
        "x": arr("L0_attn_x"),
        "w_in_t": arr("L0_attn_W_in").T,
        "conv_taps": taps,
        "wx_bc_t": w_xproj[dtr:].T,
        "wx_dt": w_xproj[:dtr],
        "w_dt_t": w_dt.T,
        "b_dt": arr("L0_attn_b_dt")[:, None],
        "a_log": a_log,
        "d_skip": arr("L0_attn_D")[:, None],
        "w_out_y": np.concatenate([w_out_t[:inner]] * 2, axis=0),
        "w_out_yz": w_out_t,
        "w12_t": w12.transpose(2, 0, 1),
        "w3_t": w3.reshape(experts, d, hidden // P, P).transpose(3, 0, 2, 1),
        "gate_t": gate_w.T,
        "select": select,
        "ident": np.eye(P, dtype=np.float32),
        "rank_key": rank_key,
    }
    arrays = {k: np.ascontiguousarray(a) for k, a in arrays.items()}
    nc = bacc.Bacc("TRN2", target_bir_lowering=False, num_devices=1)
    ins = {k: nc.dram_tensor(k, a.shape, mybir.dt.from_np(a.dtype), kind="ExternalInput").ap() for k, a in arrays.items()}
    out = nc.dram_tensor("out", arrays["x"].shape, F32, kind="ExternalOutput").ap()
    mixer_moe_kernel(nc, out=out, **ins)
    r = run_bass_kernel_spmd(nc, [arrays], core_ids=[0])
    return r.results[0]["out"]
```

```python
from contextlib import ExitStack

import concourse.bass as bass
from concourse import mybir

ALU = mybir.AluOpType
ACT = mybir.ActivationFunctionType
AX_X = mybir.AxisListType.X
F32 = mybir.dt.float32
F32R = mybir.dt.float32r

P = 128
GROUP = 512
TILES = GROUP // P
LN_EPS = 1e-5
CLIP_MIN = 1e-4
A_MIN = 1e-4
PRE_MAX = 20.0
LOWEST = -3.0e38
GATE_STEPS = 15
RSTD_STEPS = 6
MARGIN_STEP = 8


class Stage:

    def __init__(self, sem, per, base=0):
        self.sem, self.per, self.base = sem, per, base

    def at(self, window, done):
        return window * self.per + (self.base + done)


def mixer_moe_kernel(nc, x, w_in_t, conv_taps, wx_bc_t, wx_dt, w_dt_t, b_dt, a_log, d_skip, w_out_y, w_out_yz,
                     w12_t, w3_t, gate_t, select, ident, rank_key, out):
    BATCHES, L, D = x.shape
    GROUPS = L // GROUP
    EXPERTS, H2 = w12_t.shape[1:]
    HB = H2 // 2 // P
    UNITS = EXPERTS
    HALVES = HB
    INNER = w_out_yz.shape[0] // 2
    NJ = a_log.shape[1]
    DTR = wx_dt.shape[0]
    DSTATE = wx_bc_t.shape[1] // 2
    assert D == P and 2 * INNER == P and GROUPS == 2 and HB == 2

    x_v = x.rearrange("b (g t p) d -> b g p t d", g=GROUPS, p=P)
    out_v = out.rearrange("b (g t p) d -> b g p t d", g=GROUPS, p=P)

    with ExitStack() as ctx:
        def sb(name, shape, dt=F32):
            return ctx.enter_context(nc.sbuf_tensor(name, shape, dt))

        def stage(name, per, base=0):
            return Stage(ctx.enter_context(nc.semaphore(name)), per, base)

        def event(name):
            return ctx.enter_context(nc.semaphore(name))

        w12_f = sb("w12_f", [P, EXPERTS, H2])
        w12_hi = sb("w12_hi", [P, EXPERTS, H2], F32R)
        w12_lo = sb("w12_lo", [P, EXPERTS, H2], F32R)
        w3_sb = sb("w3_sb", [P, EXPERTS, HB, D])
        win_f = sb("win_f", [P, P])
        win_hi = sb("win_hi", [P, P], F32R)
        win_lo = sb("win_lo", [P, P], F32R)
        gate_f = sb("gate_f", [P, EXPERTS])
        gate_hi = sb("gate_hi", [P, EXPERTS], F32R)
        gate_lo = sb("gate_lo", [P, EXPERTS], F32R)
        sel_f = sb("sel_f", [P, 2 * NJ, P])
        sel_r = sb("sel_r", [P, 2 * NJ, P], F32R)
        id_sb = sb("id_sb", [P, P])
        key_sb = sb("key_sb", [P, TILES, EXPERTS])
        taps = sb("taps", [P, 3])
        wp = sb("wp", [INNER, P])
        wx_bc_sb = sb("wx_bc_sb", [INNER, 2 * DSTATE])
        wx_dt_sb = sb("wx_dt_sb", [DTR, INNER])
        w_dt_sb = sb("w_dt_sb", [DTR, INNER])
        b_dt_sb = sb("b_dt_sb", [INNER, 1])
        a_in = sb("a_in", [P, NJ])
        a_abs = sb("a_abs", [P, NJ])
        a_exp = sb("a_exp", [P, NJ])
        a_ln = sb("a_ln", [P, NJ])
        a_sum = sb("a_sum", [P, NJ])
        a_neg = sb("a_neg", [P, NJ])
        d_sb = sb("d_sb", [INNER, 1])
        wy_in = sb("wy_in", [P, D])
        wy_neg = sb("wy_neg", [P, D])
        wyz_in = sb("wyz_in", [P, D])
        wxz = sb("wxz", [P, D])
        power = sb("power", [P, TILES])
        quarter = sb("quarter", [P, TILES])

        WINDOWS = BATCHES * GROUPS
        x_sb = sb("x_sb", [P, WINDOWS, TILES, D])
        xt_hi = [sb(f"xt_hi{s}", [P, GROUP], F32R) for s in range(2)]
        xt_lo = [sb(f"xt_lo{s}", [P, GROUP], F32R) for s in range(2)]
        new_hi = sb("new_hi", [P, GROUP], F32R)
        new_lo = sb("new_lo", [P, GROUP], F32R)
        gates = [sb(f"gates{s}", [P, TILES, EXPERTS]) for s in range(2)]
        h_in = [sb(f"h_in{s}", [P, GROUP + 2]) for s in range(2)]

        bn = sb("bn", [P, TILES, 6])
        mean_sum = sb("mean_sum", [P, TILES])
        mean_gap = sb("mean_gap", [P, TILES])
        gap_sq = sb("gap_sq", [P, TILES])
        square_sum = sb("square_sum", [P, TILES])
        neg_mean = sb("neg_mean", [P, TILES])
        shift = sb("shift", [P, TILES])
        var_eps = sb("var_eps", [P, TILES])
        rstd = sb("rstd", [P, TILES])
        xn = sb("xn", [P, TILES, D])
        score = sb("score", [P, TILES, EXPERTS])
        score2 = sb("score2", [P, TILES, EXPERTS])
        top = [sb(f"top{n}", [P, TILES]) for n in range(2)]
        hit = [sb(f"hit{n}", [P, TILES, EXPERTS]) for n in range(2)]
        keyed = [sb(f"keyed{n}", [P, TILES, EXPERTS]) for n in range(2)]
        key_max = [sb(f"key_max{n}", [P, TILES]) for n in range(2)]
        one_hot = [sb(f"one_hot{n}", [P, TILES, EXPERTS]) for n in range(2)]
        margin = sb("margin", [P, TILES])
        lean = sb("lean", [P, TILES])
        both = sb("both", [P, TILES, EXPERTS])
        apart = sb("apart", [P, TILES, EXPERTS])
        leaned = sb("leaned", [P, TILES, EXPERTS])

        acc = [sb(f"acc{s}", [P, TILES, D]) for s in range(2)]

        g_sb = [sb(f"g_sb{a}", [P, GROUP]) for a in range(2)]
        hid = [[sb(f"hid{s}{a}", [P, GROUP]) for a in range(HALVES)] for s in range(2)]
        gated = [sb(f"gated{s}", [P, TILES, D]) for s in range(2)]

        conv = sb("conv", [P, GROUP])
        xz = sb("xz", [P, GROUP])
        xx = sb("xx", [P, GROUP])
        bc = sb("bc", [P, GROUP])
        bc_r = sb("bc_r", [P, GROUP], F32R)
        pre = sb("pre", [INNER, GROUP])
        pre_exp = sb("pre_exp", [INNER, GROUP])
        delta = sb("delta", [P, GROUP])
        decay = [sb(f"decay{j}", [P, GROUP]) for j in range(NJ)]
        bx = [sb(f"bx{j}", [P, GROUP]) for j in range(NJ)]
        state = [[sb(f"state{s}{j}", [P, GROUP]) for j in range(NJ)] for s in range(2)]
        mix = sb("mix", [P, TILES, D])

        h_ps = [ctx.enter_context(nc.psum_tensor(f"h_ps{a}", [P, 2, GROUP], F32)) for a in range(2)]
        y_ps = [ctx.enter_context(nc.psum_tensor(f"y_ps{s}", [P, TILES, D], F32)) for s in range(2)]
        s_ps = [ctx.enter_context(nc.psum_tensor(f"s_ps{s}", [P, GROUP], F32)) for s in range(2)]

        small_loaded = event("small_loaded")
        late_loaded = event("late_loaded")
        w12_loaded = [event(f"w12_loaded{e}") for e in range(EXPERTS)]
        w3_loaded = [event(f"w3_loaded{e}") for e in range(EXPERTS)]
        xt_moved = [event(f"xt_moved{s}") for s in range(2)]
        x_loaded = [event(f"x_loaded{s}") for s in range(3)]
        consts_set = event("consts_set")
        win_hi_done = event("win_hi_done")
        win_lo_done = event("win_lo_done")
        w12_hi_done = event("w12_hi_done")
        w12_lo_done = event("w12_lo_done")
        a_dve_step = event("a_dve_step")
        a_act_step = event("a_act_step")
        sel_done = event("sel_done")
        w_comb_full = event("w_comb_full")
        wp_done = event("wp_done")
        w_out_done = event("w_out_done")
        bn_done = stage("bn_done", TILES, 2 * TILES)
        rstd_step = stage("rstd_step", RSTD_STEPS, 2 * RSTD_STEPS)
        xn_done = stage("xn_done", TILES, 2 * TILES)
        xt_full = stage("xt_full", 1, 2)
        xt_hi_done = stage("xt_hi_done", 1, 2)
        xt_lo_done = stage("xt_lo_done", 1, 2)
        score_full = stage("score_full", 1, 2)
        h_in_full = stage("h_in_full", 1, 2)
        h_in_done = stage("h_in_done", 1, 2)
        score_kept = stage("score_kept", 1, 2)
        gate_stepped = stage("gate_stepped", GATE_STEPS, 2 * GATE_STEPS)
        lean_done = stage("lean_done", 1, 2)
        h_full = stage("h_full", UNITS * HALVES, 2)
        silu_done = stage("silu_done", UNITS * HALVES)
        hid_done = stage("hid_done", UNITS * HALVES, 2)
        y_full = stage("y_full", UNITS, 2)
        gated_done = stage("gated_done", UNITS, 2)
        acc_done = stage("acc_done", UNITS + 1, 2)
        acc_loaded = [event(f"acc_loaded{s}") for s in range(2)]
        out_stored = [event(f"out_stored{s}") for s in range(2)]
        conv_stepped = stage("conv_stepped", 3)
        xz_done = stage("xz_done", 3)
        proj_full = stage("proj_full", 1)
        bc_tanh_done = stage("bc_tanh_done", 1)
        pre_done = stage("pre_done", 1)
        bc_split = stage("bc_split", 2)
        bc_full = stage("bc_full", 2 * NJ)
        softplus_step = stage("softplus_step", 2)
        delta_done = stage("delta_done", 1)
        decay_done = stage("decay_done", NJ)
        clip_done = stage("clip_done", NJ)
        bx_done = stage("bx_done", NJ)
        drive_done = stage("drive_done", NJ)
        scan_done = stage("scan_done", NJ)
        c_state_done = stage("c_state_done", NJ)
        state_sum_step = stage("state_sum_step", NJ - 1)
        mix_full = stage("mix_full", 1)
        mix_done = stage("mix_done", 1, 1)

        block = ctx.enter_context(nc.Block())

        USES = (["proj", "bc0", "bc1", "xt", "bc2", "bc3", "score", "h_in"]
                + [f"bc{n}" for n in range(NJ, 2 * NJ)] + ["mix"])
        FIRST_USES = ["xt-2", "score-2", "h_in-2", "xt-1", "score-1", "h_in-1"]

        def bank(g, use):
            return s_ps[(g * len(USES) + USES.index(use)) % 2]

        def first_bank(use):
            return s_ps[FIRST_USES.index(use) % 2]


        def flat(t):
            return t[:, :, :].rearrange("p t d -> p (t d)")

        comb_ps = flat(y_ps[1])

        SMALL = ((id_sb, ident), (win_f, w_in_t), (gate_f, gate_t), (key_sb, rank_key))
        LATE = ((sel_f, select), (taps, conv_taps), (wx_dt_sb, wx_dt), (w_dt_sb, w_dt_t), (b_dt_sb, b_dt),
                (a_in, a_log), (d_sb, d_skip), (wy_in, w_out_y), (wyz_in, w_out_yz), (wx_bc_sb, wx_bc_t))

        @block.sync
        def _(sp):
            def load_expert(e):
                sp.dma_start(w12_f[:, e, :], w12_t[:, e, :]).then_inc(w12_loaded[e], 16)
                sp.dma_start(w3_sb[:, e, :, :], w3_t[:, e, :, :]).then_inc(w3_loaded[e], 16)

            sp.dma_start(x_sb[:, 0, :, :], x_v[0, 0]).then_inc(x_loaded[0], 16)
            for dst, src in SMALL:
                sp.dma_start(dst[:], src).then_inc(small_loaded, 16)
            sp.dma_start(x_sb[:, 1, :, :], x_v[0, 1]).then_inc(x_loaded[1], 16)
            load_expert(0)
            for dst, src in LATE:
                sp.dma_start(dst[:], src).then_inc(late_loaded, 16)
            load_expert(1)
            for n in range(GROUPS, WINDOWS):
                sp.dma_start(x_sb[:, n, :, :], x_v[n // GROUPS, n % GROUPS]).then_inc(x_loaded[2], 16)
            for e in range(2, EXPERTS):
                load_expert(e)
            with sp.Fori(0, BATCHES) as i:
                for g in range(GROUPS):
                    w = i * GROUPS + g
                    sp.wait_ge(x_loaded[2], 16 * (WINDOWS - GROUPS))
                    sp.wait_ge(x_loaded[g], 16)
                    sp.wait_ge(out_stored[g], 16 * i + 16)
                    sp.dma_start(acc[g][:, :, :], x_sb[:, w, :, :]).then_inc(acc_loaded[g], 16)
                    sp.wait_ge(xt_lo_done.sem, xt_lo_done.at(w - 1, 1))
                    sp.wait_ge(h_full.sem, h_full.at(w, 0))
                    sp.dma_start(xt_hi[1 - g][:, :].bitcast(F32), new_hi[:, :].bitcast(F32)).then_inc(xt_moved[1 - g], 16)
                    sp.dma_start(xt_lo[1 - g][:, :].bitcast(F32), new_lo[:, :].bitcast(F32)).then_inc(xt_moved[1 - g], 16)
                    sp.wait_ge(acc_done.sem, acc_done.at(w, UNITS + 1))
                    sp.dma_start(out_v[i, g], acc[g][:, :, :]).then_inc(out_stored[g], 16)
            for g in range(GROUPS):
                sp.wait_ge(out_stored[g], 16 * (BATCHES + 1))
            sp.wait_ge(xt_moved[0], 32 * (BATCHES + 1))
            sp.wait_ge(xt_moved[1], 32 * BATCHES)

        @block.gpsimd
        def _(pool):
            for st in (h_full, hid_done, y_full, gated_done, acc_done, mix_done):
                pool.sem_inc(st.sem, st.base)
            for s in range(2):
                pool.sem_inc(out_stored[s], 16)
            pool.sem_inc(xt_moved[0], 32)
            nc.gpsimd.memset(wp[:, :], 0.0).then_inc(consts_set, 1)
            nc.gpsimd.memset(power[:, :], -0.5).then_inc(consts_set, 1)
            nc.gpsimd.memset(quarter[:, :], 0.25).then_inc(consts_set, 1)
            nc.gpsimd.memset(h_in[0][:, 0:1], 0.0).then_inc(consts_set, 1)
            nc.gpsimd.memset(h_in[1][:, GROUP + 1:GROUP + 2], 0.0).then_inc(consts_set, 1)
            pool.wait_ge(consts_set, 5)

            def inverse_deviation(w, first=False):
                even, odd = bn[:, :, 0:3], bn[:, :, 3:6]
                pool.wait_ge(bn_done.sem, bn_done.at(w, TILES))
                nc.gpsimd.tensor_tensor(mean_sum[:, :], even[:, :, 1], odd[:, :, 1], ALU.add)
                nc.gpsimd.tensor_tensor(mean_gap[:, :], even[:, :, 1], odd[:, :, 1], ALU.subtract)
                nc.gpsimd.tensor_tensor(square_sum[:, :], even[:, :, 2], odd[:, :, 2], ALU.add).then_inc(rstd_step.sem, 1)
                pool.wait_ge(rstd_step.sem, rstd_step.at(w, 1))
                nc.gpsimd.tensor_tensor(gap_sq[:, :], mean_gap[:, :], mean_gap[:, :], ALU.mult)
                nc.gpsimd.tensor_scalar(neg_mean[:, :], mean_sum[:, :], -0.5, 0.0, ALU.mult, ALU.add)
                nc.gpsimd.tensor_scalar(square_sum[:, :], square_sum[:, :], 1.0 / D, LN_EPS, ALU.mult, ALU.add).then_inc(rstd_step.sem, 1)
                pool.wait_ge(rstd_step.sem, rstd_step.at(w, 2))
                nc.gpsimd.tensor_tensor(gap_sq[:, :], gap_sq[:, :], quarter[:, :], ALU.mult).then_inc(rstd_step.sem, 1)
                pool.wait_ge(rstd_step.sem, rstd_step.at(w, 3))
                nc.gpsimd.tensor_tensor(var_eps[:, :], square_sum[:, :], gap_sq[:, :], ALU.add).then_inc(rstd_step.sem, 1)
                if not first:
                    pool.wait_ge(xn_done.sem, xn_done.at(w - 1, TILES))
                pool.wait_ge(rstd_step.sem, rstd_step.at(w, 4))
                nc.gpsimd.tensor_tensor(rstd[:, :], var_eps[:, :], power[:, :], ALU.pow).then_inc(rstd_step.sem, 1)
                pool.wait_ge(rstd_step.sem, rstd_step.at(w, 5))
                nc.gpsimd.tensor_tensor(shift[:, :], neg_mean[:, :], rstd[:, :], ALU.mult).then_inc(rstd_step.sem, 1)

            inverse_deviation(-2, True)
            inverse_deviation(-1)
            with pool.Fori(0, BATCHES) as i:
                for g in range(GROUPS):
                    w = i * GROUPS + g

                    def add_expert(u):
                        pool.wait_ge(gated_done.sem, gated_done.at(w, u + 1))
                        if u > 0:
                            pool.wait_ge(acc_done.sem, acc_done.at(w, u))
                        else:
                            pool.wait_ge(acc_loaded[g], 16 * i + 16)
                        nc.gpsimd.tensor_tensor(flat(acc[g]), flat(acc[g]), flat(gated[u % 2]),
                                                ALU.add).then_inc(acc_done.sem, 1)

                    def add_tile(j):
                        pool.wait_ge(c_state_done.sem, c_state_done.at(w, j + 1))
                        if j > 1:
                            pool.wait_ge(state_sum_step.sem, state_sum_step.at(w, j - 1))
                        nc.gpsimd.tensor_tensor(bx[0][:, :], bx[0][:, :], bx[j][:, :], ALU.add).then_inc(state_sum_step.sem, 1)

                    def clip_decay(j):
                        nc.gpsimd.tensor_scalar(decay[j][:, :], decay[j][:, :], CLIP_MIN, 1.0, ALU.max, ALU.min).then_inc(clip_done.sem, 1)

                    inverse_deviation(w)
                    for u in range(UNITS):
                        if u == 2:
                            pool.wait_ge(decay_done.sem, decay_done.at(w, NJ))
                        if u == 6:
                            add_tile(1)
                            add_tile(2)
                            add_tile(3)
                        add_expert(u)
                        if u == 2:
                            clip_decay(0)
                            clip_decay(1)
                            clip_decay(2)
                            clip_decay(3)
                    pool.wait_ge(mix_done.sem, mix_done.at(w, 1))
                    pool.wait_ge(acc_done.sem, acc_done.at(w, UNITS))
                    nc.gpsimd.tensor_tensor(flat(acc[g]), flat(acc[g]), flat(mix), ALU.add).then_inc(acc_done.sem, 1)

        @block.scalar
        def _(act):
            def keep_xt_hi(w, hi, ps):
                act.wait_ge(xt_full.sem, xt_full.at(w, 1))
                nc.scalar.copy(hi[:, :], ps[:, :]).then_inc(xt_hi_done.sem, 1)

            def normalise(w, x_ap):
                act.wait_ge(rstd_step.sem, rstd_step.at(w, RSTD_STEPS))
                for t in range(TILES):
                    nc.scalar.activation(xn[:, t, :], x_ap[:, t, :], ACT.Identity, bias=shift[:, t:t + 1],
                                         scale=rstd[:, t:t + 1]).then_inc(xn_done.sem, 1)

            def keep_scores(w, ps, first=False):
                act.wait_ge(score_full.sem, score_full.at(w, 1))
                if not first:
                    act.wait_ge(gate_stepped.sem, gate_stepped.at(w - 1, GATE_STEPS))
                nc.scalar.copy(flat(score), ps[:, 0:TILES * EXPERTS]).then_inc(score_kept.sem, 1)

            def keep_h_in(w, slot, ps, halo):
                act.wait_ge(h_in_full.sem, h_in_full.at(w, 1))
                last = nc.scalar.copy(h_in[slot][:, 1:GROUP + 1], ps[:, :])
                if halo:
                    nc.scalar.copy(h_in[0][:, GROUP + 1:GROUP + 2], ps[:, 0:1])
                    last = nc.scalar.copy(h_in[1][:, 0:1], h_in[0][:, GROUP:GROUP + 1])
                last.then_inc(h_in_done.sem, 1)

            def lean_to_best(w):
                act.wait_ge(gate_stepped.sem, gate_stepped.at(w, MARGIN_STEP))
                nc.scalar.activation(lean[:, :], margin[:, :], ACT.Tanh, scale=0.5).then_inc(lean_done.sem, 1)

            normalise(-2, x_sb[:, 0])
            keep_xt_hi(-2, xt_hi[0], first_bank("xt-2"))
            normalise(-1, x_sb[:, 1])
            act.wait_ge(small_loaded, 16 * len(SMALL))
            nc.scalar.copy(win_hi[:, :], win_f[:, :])
            nc.scalar.copy(gate_hi[:, :], gate_f[:, :]).then_inc(win_hi_done, 1)
            act.wait_ge(w12_loaded[0], 16)
            nc.scalar.copy(w12_hi[:, 0, :], w12_f[:, 0, :]).then_inc(w12_hi_done, 1)
            keep_scores(-2, first_bank("score-2"), True)
            keep_h_in(-2, 0, first_bank("h_in-2"), False)
            keep_xt_hi(-1, new_hi, first_bank("xt-1"))
            keep_h_in(-1, 1, first_bank("h_in-1"), True)
            act.wait_ge(late_loaded, 16 * len(LATE))
            nc.scalar.copy(sel_r[INNER:P, :, :], sel_f[INNER:P, :, :]).then_inc(sel_done, 1)
            act.wait_ge(consts_set, 1)
            for at in (INNER, INNER + 32):
                nc.scalar.copy(wp[:, at:at + 2 * DSTATE], wx_bc_sb[:, :])
            act.wait_ge(w_comb_full, 1)
            nc.scalar.copy(wp[:, 0:INNER], comb_ps[0:INNER, 0:INNER]).then_inc(wp_done, 1)
            nc.scalar.preload_act_table_set("natural_log_exp_and_others")
            act.wait_ge(a_dve_step, 1)
            nc.scalar.activation(a_exp[:, :], a_abs[:, :], ACT.Exp, scale=-1.0).then_inc(a_act_step, 1)
            act.wait_ge(a_act_step, 1)
            nc.scalar.activation(a_ln[:, :], a_exp[:, :], ACT.Ln, bias=1.0).then_inc(a_act_step, 1)
            nc.scalar.preload_act_table_set("silu_and_others")
            for e in range(1, EXPERTS):
                act.wait_ge(w12_loaded[e], 16)
                nc.scalar.copy(w12_hi[:, e, :], w12_f[:, e, :]).then_inc(w12_hi_done, 1)
            lean_to_best(-2)
            keep_scores(-1, first_bank("score-1"))
            lean_to_best(-1)

            with act.Fori(0, BATCHES) as i:
                for g in range(GROUPS):
                    w = i * GROUPS + g
                    new = ((i + 1) % BATCHES) * GROUPS + g

                    def first_tap():
                        act.wait_ge(h_in_done.sem, h_in_done.at(w - 1, 1))
                        nc.scalar.activation(conv[:, :], h_in[g][:, 0:GROUP], ACT.Copy, scale=taps[:, 0:1]).then_inc(conv_stepped.sem, 1)

                    def keep_mix():
                        act.wait_ge(mix_full.sem, mix_full.at(w, 1))
                        nc.scalar.copy(flat(mix), bank(g, "mix")[:, :]).then_inc(mix_done.sem, 1)

                    def silu(u, a):
                        act.wait_ge(h_full.sem, h_full.at(w, HALVES * u + a + 1))
                        nc.scalar.activation(g_sb[a][:, :], h_ps[a][:, 0, :], ACT.Silu).then_inc(silu_done.sem, 1)

                    def conv_silu():
                        act.wait_ge(conv_stepped.sem, conv_stepped.at(w, 3))
                        nc.scalar.activation(xz[:, :], conv[:, :], ACT.Silu).then_inc(xz_done.sem, 1)
                        nc.scalar.activation(xx[0:INNER, :], conv[0:INNER, :], ACT.Silu).then_inc(xz_done.sem, 1)
                        nc.scalar.activation(xx[INNER:P, :], conv[0:INNER, :], ACT.Silu).then_inc(xz_done.sem, 1)

                    def bc_tanh():
                        act.wait_ge(proj_full.sem, proj_full.at(w, 1))
                        nc.scalar.activation(bc[INNER:P, :], bank(g, "proj")[INNER:P, :], ACT.Tanh).then_inc(bc_tanh_done.sem, 1)
                        act.wait_ge(bc_tanh_done.sem, bc_tanh_done.at(w, 1))
                        nc.scalar.copy(bc_r[INNER:P, :], bc[INNER:P, :]).then_inc(bc_split.sem, 1)

                    def softplus():
                        act.wait_ge(pre_done.sem, pre_done.at(w, 1))
                        nc.scalar.activation(pre_exp[:, :], pre[:, :], ACT.Exp).then_inc(softplus_step.sem, 1)
                        act.wait_ge(softplus_step.sem, softplus_step.at(w, 1))
                        nc.scalar.activation(pre_exp[:, :], pre_exp[:, :], ACT.Ln, bias=1.0).then_inc(softplus_step.sem, 1)

                    def decay_exp():
                        act.wait_ge(delta_done.sem, delta_done.at(w, 1))
                        for j in range(NJ):
                            nc.scalar.activation(decay[j][:, :], delta[:, :], ACT.Exp, scale=a_neg[:, j:j + 1]).then_inc(decay_done.sem, 1)

                    first_tap()
                    for u in range(UNITS):
                        silu(u, 0)
                        if u == 0:
                            conv_silu()
                        silu(u, 1)
                        if u == 0:
                            normalise(w, x_sb[:, new])
                        if u == 1:
                            bc_tanh()
                        if u == 2:
                            nc.scalar.preload_act_table_set("natural_log_exp_and_others")
                            softplus()
                            act.wait_ge(xt_moved[1 - g], 32 * (i + 1 + g))
                            keep_xt_hi(w, new_hi, bank(g, "xt"))
                            decay_exp()
                            nc.scalar.preload_act_table_set("silu_and_others")
                        if u == 3:
                            keep_scores(w, bank(g, "score"))
                            keep_h_in(w, g, bank(g, "h_in"), g == 1)
                        if u == 6:
                            lean_to_best(w)
                    keep_mix()

        @block.vector
        def _(dve):
            def statistics(w, x_ap):
                for t in range(TILES):
                    nc.vector.bn_stats(bn[:, t, :], x_ap[:, t, :]).then_inc(bn_done.sem, 1)

            def keep_xt_lo(w, hi, lo, ps):
                dve.wait_ge(xt_hi_done.sem, xt_hi_done.at(w, 1))
                nc.vector.tensor_tensor(lo[:, :], ps[:, :], hi[:, :].bitcast(F32), ALU.subtract).then_inc(xt_lo_done.sem, 1)

            def wide(t):
                return t[:, :].unsqueeze(2).to_broadcast([P, TILES, EXPERTS])

            def gate_step(w, slot, n):
                if n == 1:
                    dve.wait_ge(score_kept.sem, score_kept.at(w, 1))
                else:
                    dve.wait_ge(gate_stepped.sem, gate_stepped.at(w, n - 1))
                k, from_, m = (0, score, n - 1) if n < 6 else (1, score2, n - 7 if n < 9 else n - 8)
                if n == 6:
                    last = nc.vector.scalar_tensor_tensor(out=score2[:, :, :], in0=one_hot[0][:, :, :], scalar=LOWEST,
                                                          in1=score[:, :, :], op0=ALU.mult, op1=ALU.add)
                elif n == MARGIN_STEP:
                    last = nc.vector.tensor_tensor(margin[:, :], top[0][:, :], top[1][:, :], ALU.subtract)
                elif n == 13:
                    nc.vector.tensor_tensor(both[:, :, :], one_hot[0][:, :, :], one_hot[1][:, :, :], ALU.add)
                    last = nc.vector.tensor_tensor(apart[:, :, :], one_hot[0][:, :, :], one_hot[1][:, :, :], ALU.subtract)
                elif n == 14:
                    dve.wait_ge(lean_done.sem, lean_done.at(w, 1))
                    last = nc.vector.scalar_tensor_tensor(out=leaned[:, :, :], in0=apart[:, :, :], scalar=0.5,
                                                          in1=wide(lean), op0=ALU.mult, op1=ALU.mult)
                elif n == 15:
                    last = nc.vector.scalar_tensor_tensor(out=gates[slot][:, :, :], in0=both[:, :, :], scalar=0.5,
                                                          in1=leaned[:, :, :], op0=ALU.mult, op1=ALU.add)
                elif m == 0:
                    last = nc.vector.tensor_reduce(top[k][:, :], from_[:, :, :], AX_X, ALU.max)
                elif m == 1:
                    last = nc.vector.tensor_tensor(hit[k][:, :, :], from_[:, :, :], wide(top[k]), ALU.is_equal)
                elif m == 2:
                    last = nc.vector.tensor_tensor(keyed[k][:, :, :], hit[k][:, :, :], key_sb[:, :, :], ALU.mult)
                elif m == 3:
                    last = nc.vector.tensor_reduce(key_max[k][:, :], keyed[k][:, :, :], AX_X, ALU.max)
                elif m == 4:
                    last = nc.vector.tensor_tensor(one_hot[k][:, :, :], keyed[k][:, :, :], wide(key_max[k]), ALU.is_equal)
                last.then_inc(gate_stepped.sem, 1)

            dve.wait_ge(x_loaded[0], 16)
            statistics(-2, x_sb[:, 0])
            dve.wait_ge(x_loaded[1], 16)
            dve.wait_ge(rstd_step.sem, 1)
            statistics(-1, x_sb[:, 1])
            keep_xt_lo(-2, xt_hi[0], xt_lo[0], first_bank("xt-2"))
            dve.wait_ge(win_hi_done, 1)
            nc.vector.tensor_tensor(win_lo[:, :], win_f[:, :], win_hi[:, :].bitcast(F32), ALU.subtract)
            nc.vector.tensor_tensor(gate_lo[:, :], gate_f[:, :], gate_hi[:, :].bitcast(F32), ALU.subtract).then_inc(win_lo_done, 1)
            dve.wait_ge(w12_hi_done, 1)
            nc.vector.tensor_tensor(w12_lo[:, 0, :], w12_f[:, 0, :], w12_hi[:, 0, :].bitcast(F32), ALU.subtract).then_inc(w12_lo_done, 1)
            keep_xt_lo(-1, new_hi, new_lo, first_bank("xt-1"))
            dve.wait_ge(late_loaded, 16 * len(LATE))
            nc.vector.scalar_tensor_tensor(out=a_abs[:, :], in0=a_in[:, :], scalar=-1.0, in1=a_in[:, :],
                                           op0=ALU.mult, op1=ALU.max).then_inc(a_dve_step, 1)
            nc.vector.tensor_scalar(wy_neg[:, :], wy_in[:, :], -1.0, None, ALU.mult).then_inc(w_out_done, 1)
            nc.vector.tensor_scalar(wxz[0:INNER, :], wyz_in[0:INNER, :], d_sb[:, 0:1], None, ALU.mult).then_inc(w_out_done, 1)
            nc.vector.tensor_copy(wxz[INNER:P, :], wyz_in[INNER:P, :]).then_inc(w_out_done, 1)
            dve.wait_ge(a_act_step, 2)
            nc.vector.scalar_tensor_tensor(out=a_sum[:, :], in0=a_in[:, :], scalar=0.0, in1=a_ln[:, :],
                                           op0=ALU.max, op1=ALU.add).then_inc(a_dve_step, 1)
            dve.wait_ge(a_dve_step, 2)
            nc.vector.tensor_scalar(a_neg[:, :], a_sum[:, :], A_MIN, -1.0, ALU.add, ALU.mult).then_inc(a_dve_step, 1)
            for e in range(1, EXPERTS):
                dve.wait_ge(w12_hi_done, e + 1)
                nc.vector.tensor_tensor(w12_lo[:, e, :], w12_f[:, e, :], w12_hi[:, e, :].bitcast(F32), ALU.subtract).then_inc(w12_lo_done, 1)
                for n in range(2 * e - 1, 2 * e + 1):
                    gate_step(-2, 0, n)
            gate_step(-2, 0, GATE_STEPS)
            for n in range(1, GATE_STEPS + 1):
                gate_step(-1, 1, n)

            with dve.Fori(0, BATCHES) as i:
                for g in range(GROUPS):
                    w = i * GROUPS + g
                    new = ((i + 1) % BATCHES) * GROUPS + g

                    def product(u, a):
                        dve.wait_ge(silu_done.sem, silu_done.at(w, HALVES * u + a + 1))
                        dve.wait_ge(y_full.sem, y_full.at(w, u - 1))
                        nc.vector.tensor_tensor(hid[u % 2][a][:, :], h_ps[a][:, 1, :], g_sb[a][:, :], ALU.mult).then_inc(hid_done.sem, 1)

                    def gate(u):
                        dve.wait_ge(y_full.sem, y_full.at(w, u + 1))
                        dve.wait_ge(acc_done.sem, acc_done.at(w, u - 1 if u > 1 else u - 2))
                        if u == 0:
                            dve.wait_ge(gate_stepped.sem, gate_stepped.at(w - 2, GATE_STEPS))
                        nc.vector.tensor_tensor(gated[u % 2][:, :, :], y_ps[u % 2][:, :, :],
                                                gates[g][:, :, u].unsqueeze(2).to_broadcast([P, TILES, D]), ALU.mult).then_inc(gated_done.sem, 1)

                    def convolve():
                        for k in range(1, 3):
                            dve.wait_ge(conv_stepped.sem, conv_stepped.at(w, k))
                            nc.vector.scalar_tensor_tensor(out=conv[:, :], in0=h_in[g][:, k:k + GROUP], scalar=taps[:, k:k + 1],
                                                           in1=conv[:, :], op0=ALU.mult, op1=ALU.add).then_inc(conv_stepped.sem, 1)

                    def keep_pre():
                        dve.wait_ge(proj_full.sem, proj_full.at(w, 1))
                        nc.vector.tensor_scalar(pre[:, :], bank(g, "proj")[0:INNER, :], b_dt_sb[:, 0:1], PRE_MAX,
                                                ALU.add, ALU.min).then_inc(pre_done.sem, 1)

                    def split_bc():
                        dve.wait_ge(bc_split.sem, bc_split.at(w, 1))
                        nc.vector.tensor_tensor(bc_r[INNER + 32:P, :], bc[INNER + 32:P, :], bc_r[INNER + 32:P, :].bitcast(F32),
                                                ALU.subtract).then_inc(bc_split.sem, 1)

                    def b_times_x(j):
                        dve.wait_ge(bc_full.sem, bc_full.at(w, j + 1))
                        if j == 0:
                            dve.wait_ge(xz_done.sem, xz_done.at(w, 3))
                        nc.vector.tensor_tensor(bx[j][:, :], bank(g, f"bc{j}")[:, :], xx[:, :], ALU.mult).then_inc(bx_done.sem, 1)

                    def clip_delta():
                        dve.wait_ge(softplus_step.sem, softplus_step.at(w, 2))
                        nc.vector.tensor_scalar(delta[0:INNER, :], pre_exp[:, :], CLIP_MIN, 1.0, ALU.max, ALU.min)
                        nc.vector.tensor_scalar(delta[INNER:P, :], pre_exp[:, :], CLIP_MIN, 1.0, ALU.max, ALU.min).then_inc(delta_done.sem, 1)

                    def negative_drive(j):
                        dve.wait_ge(clip_done.sem, clip_done.at(w, j + 1))
                        dve.wait_ge(bx_done.sem, bx_done.at(w, j + 1))
                        nc.vector.scalar_tensor_tensor(out=bx[j][:, :], in0=decay[j][:, :], scalar=1.0, in1=bx[j][:, :],
                                                       op0=ALU.subtract, op1=ALU.mult).then_inc(drive_done.sem, 1)

                    def scan(j):
                        dve.wait_ge(drive_done.sem, drive_done.at(w, j + 1))
                        first = 0.0 if g == 0 else state[0][j][:, GROUP - 1:GROUP]
                        nc.vector.tensor_tensor_scan(state[g][j][:, :], decay[j][:, :], bx[j][:, :], first, ALU.mult, ALU.add).then_inc(scan_done.sem, 1)

                    def c_times_state(j):
                        dve.wait_ge(bc_full.sem, bc_full.at(w, NJ + j + 1))
                        dve.wait_ge(scan_done.sem, scan_done.at(w, j + 1))
                        nc.vector.tensor_tensor(bx[j][:, :], bank(g, f"bc{NJ + j}")[:, :], state[g][j][:, :], ALU.mult).then_inc(c_state_done.sem, 1)

                    def new_gate(first, end):
                        for n in range(first, end):
                            gate_step(w, g, n)

                    convolve()
                    dve.wait_ge(x_loaded[2], 16 * (WINDOWS - GROUPS))
                    statistics(w, x_sb[:, new])
                    for u in range(UNITS):
                        if u == 3:
                            keep_xt_lo(w, new_hi, new_lo, bank(g, "xt"))
                            b_times_x(2)
                            gate(2)
                            b_times_x(3)
                        product(u, 0)
                        if u == 2:
                            b_times_x(0)
                        if u == 4:
                            negative_drive(0)
                        if u == 5:
                            scan(1)
                        if u == 6:
                            c_times_state(0)
                        if u == 7:
                            c_times_state(3)
                        product(u, 1)
                        if u == 1:
                            keep_pre()
                        if u == 2:
                            b_times_x(1)
                        if u == 4:
                            scan(0)
                        if u == 5:
                            negative_drive(2)
                        if u == 6:
                            c_times_state(1)
                        if u in (1, 2, 4, 5, 6, 7):
                            gate(u - 1)
                        if u == 1:
                            split_bc()
                        if u == 2:
                            clip_delta()
                        if u == 4:
                            negative_drive(1)
                            new_gate(1, 4)
                        if u == 5:
                            scan(2)
                            negative_drive(3)
                            scan(3)
                        if u == 6:
                            c_times_state(2)
                            new_gate(4, 9)
                        if u == 7:
                            new_gate(9, 14)
                    gate(UNITS - 1)
                    new_gate(14, GATE_STEPS + 1)

        @block.tensor
        def _(pe):
            def transpose_xn(w, ps):
                pe.wait_ge(xn_done.sem, xn_done.at(w, TILES))
                for t in range(TILES):
                    last = nc.tensor.transpose(ps[:, t * P:(t + 1) * P], xn[:, t, :], id_sb[:, :])
                last.then_inc(xt_full.sem, 1)

            def three_pass(out_ps, left_hi, left_lo, right_hi, right_lo):
                nc.tensor.matmul(out_ps, left_lo, right_hi, start=True, stop=False)
                nc.tensor.matmul(out_ps, left_hi, right_lo, start=False, stop=False)
                return nc.tensor.matmul(out_ps, left_hi, right_hi, start=False, stop=True)

            def scores(w, hi, lo, ps):
                pe.wait_ge(xt_lo_done.sem, xt_lo_done.at(w, 1))
                for t in range(TILES):
                    c = slice(t * P, (t + 1) * P)
                    last = three_pass(ps[:, t * EXPERTS:(t + 1) * EXPERTS], hi[:, c], lo[:, c],
                                      gate_hi[:, :], gate_lo[:, :])
                last.then_inc(score_full.sem, 1)

            def project_in(w, hi, lo, ps):
                three_pass(ps[:, :], win_hi[:, :], win_lo[:, :], hi[:, :], lo[:, :]).then_inc(h_in_full.sem, 1)

            pe.wait_ge(small_loaded, 16 * len(SMALL))
            transpose_xn(-2, first_bank("xt-2"))
            pe.wait_ge(win_lo_done, 1)
            scores(-2, xt_hi[0], xt_lo[0], first_bank("score-2"))
            project_in(-2, xt_hi[0], xt_lo[0], first_bank("h_in-2"))
            pe.wait_ge(score_kept.sem, score_kept.at(-2, 1))
            transpose_xn(-1, first_bank("xt-1"))
            pe.wait_ge(h_in_done.sem, h_in_done.at(-2, 1))
            scores(-1, new_hi, new_lo, first_bank("score-1"))
            project_in(-1, new_hi, new_lo, first_bank("h_in-1"))
            pe.wait_ge(late_loaded, 16 * len(LATE))
            nc.tensor.matmul(comb_ps[0:INNER, 0:INNER], wx_dt_sb[:, :], w_dt_sb[:, :], start=True, stop=True).then_inc(w_comb_full, 1)
            pe.wait_ge(wp_done, 1)
            pe.wait_ge(h_in_done.sem, h_in_done.at(-1, 1))
            pe.wait_ge(score_kept.sem, score_kept.at(-1, 1))
            pe.wait_ge(sel_done, 1)
            pe.wait_ge(w_out_done, 3)

            with pe.Fori(0, BATCHES) as i:
                for g in range(GROUPS):
                    w = i * GROUPS + g

                    def hidden(u, a):
                        if g == 0 and a == 0:
                            pe.wait_ge(w12_lo_done, u + 1)
                        if u == 0 and a == 0:
                            pe.wait_ge(xt_moved[g], 32 * i + 32)
                        pe.wait_ge(hid_done.sem, hid_done.at(w, HALVES * u + a - 1))
                        for part in range(2):
                            c = slice((part * HALVES + a) * P, (part * HALVES + a + 1) * P)
                            last = three_pass(h_ps[a][:, part, :], w12_hi[:, u, c], w12_lo[:, u, c], xt_hi[g][:, :], xt_lo[g][:, :])
                        last.then_inc(h_full.sem, 1)

                    def expert_out(u):
                        if g == 0:
                            pe.wait_ge(w3_loaded[u], 16)
                        pe.wait_ge(hid_done.sem, hid_done.at(w, HALVES * (u + 1)))
                        pe.wait_ge(gated_done.sem, gated_done.at(w, u - 1))
                        for t in range(TILES):
                            for a in range(HALVES):
                                last = nc.tensor.matmul(y_ps[u % 2][:, t, :], hid[u % 2][a][:, t * P:(t + 1) * P], w3_sb[:, u, a, :],
                                                        start=(a == 0), stop=(a == HALVES - 1))
                        last.then_inc(y_full.sem, 1)

                    def project():
                        pe.wait_ge(xz_done.sem, xz_done.at(w, 1))
                        nc.tensor.matmul(bank(g, "proj")[:, :], wp[:, :], xz[0:INNER, :], start=True, stop=True).then_inc(proj_full.sem, 1)

                    def spread(n):
                        if n == 0:
                            pe.wait_ge(bc_split.sem, bc_split.at(w, 2))
                            pe.wait_ge(mix_done.sem, mix_done.at(w - 1, 1))
                        elif n == 1:
                            pe.wait_ge(pre_done.sem, pre_done.at(w, 1))
                        elif n == 2:
                            pe.wait_ge(bx_done.sem, bx_done.at(w, 2))
                        elif n == 3:
                            pe.wait_ge(xt_lo_done.sem, xt_lo_done.at(w, 1))
                        elif n == NJ:
                            pe.wait_ge(score_kept.sem, score_kept.at(w, 1))
                        elif n == NJ + 1:
                            pe.wait_ge(h_in_done.sem, h_in_done.at(w, 1))
                        else:
                            pe.wait_ge(c_state_done.sem, c_state_done.at(w, n - NJ - 1))
                        nc.tensor.matmul(bank(g, f"bc{n}")[:, :], sel_r[INNER:P, n, :], bc_r[INNER:P, :], start=True, stop=True).then_inc(bc_full.sem, 1)

                    def project_out():
                        pe.wait_ge(state_sum_step.sem, state_sum_step.at(w, 3))
                        for t in range(TILES):
                            c = slice(t * P, (t + 1) * P)
                            nc.tensor.matmul(bank(g, "mix")[:, c], bx[0][:, c], wy_neg[:, :], start=True, stop=False)
                            last = nc.tensor.matmul(bank(g, "mix")[:, c], xz[:, c], wxz[:, :], start=False, stop=True)
                        last.then_inc(mix_full.sem, 1)

                    for u in range(UNITS):
                        if u == 3:
                            pe.wait_ge(bx_done.sem, bx_done.at(w, 1))
                            transpose_xn(w, bank(g, "xt"))
                        hidden(u, 0)
                        if u == 1:
                            project()
                        if u == 2:
                            spread(0)
                        if u == 6:
                            spread(NJ + 1)
                        if u == 7:
                            spread(NJ + 3)
                        hidden(u, 1)
                        if u == 2:
                            spread(1)
                        if u == 3:
                            spread(2)
                        if u > 0:
                            expert_out(u - 1)
                        if u == 3:
                            spread(3)
                            pe.wait_ge(bx_done.sem, bx_done.at(w, 3))
                            scores(w, new_hi, new_lo, bank(g, "score"))
                            pe.wait_ge(bx_done.sem, bx_done.at(w, 4))
                            project_in(w, new_hi, new_lo, bank(g, "h_in"))
                        if u == 5:
                            spread(NJ)
                        if u == 6:
                            spread(NJ + 2)
                        if u == 7:
                            project_out()
                    expert_out(UNITS - 1)


def kernel(**inputs):
    import numpy as np
    import concourse.bacc as bacc
    from concourse.bass_utils import run_bass_kernel_spmd

    def arr(name):
        return np.asarray(inputs[name])

    w_xproj = arr("L0_attn_W_xproj")
    w_dt = arr("L0_attn_W_dt")
    inner, dtr = w_dt.shape
    dstate = (w_xproj.shape[0] - dtr) // 2
    w_out_t = arr("L0_attn_W_out").T
    w12, w3, gate_w = arr("L0_ffn_w12"), arr("L0_ffn_w3"), arr("L0_ffn_gate_w")
    experts, d, hidden = w3.shape
    nj = dstate * inner // P
    a_log = arr("L0_attn_A_log").T.reshape(nj, P).T
    taps = np.concatenate([arr("L0_attn_Kx")[:, 0, :], arr("L0_attn_Kz")[:, 0, :]], axis=0)
    select = np.zeros((P, 2 * nj, P), np.float32)
    for n in range(2 * nj):
        for member in range(2):
            row = (n // nj) * dstate + 2 * (n % nj) + member
            for copy in (inner, inner + 32):
                select[copy + row, n, member * inner:(member + 1) * inner] = 1.0
    rank_key = np.broadcast_to(np.arange(experts, 0, -1, dtype=np.float32), (P, TILES, experts))
    arrays = {
        "x": arr("L0_attn_x"),
        "w_in_t": arr("L0_attn_W_in").T,
        "conv_taps": taps,
        "wx_bc_t": w_xproj[dtr:].T,
        "wx_dt": w_xproj[:dtr],
        "w_dt_t": w_dt.T,
        "b_dt": arr("L0_attn_b_dt")[:, None],
        "a_log": a_log,
        "d_skip": arr("L0_attn_D")[:, None],
        "w_out_y": np.concatenate([w_out_t[:inner]] * 2, axis=0),
        "w_out_yz": w_out_t,
        "w12_t": w12.transpose(2, 0, 1),
        "w3_t": w3.reshape(experts, d, hidden // P, P).transpose(3, 0, 2, 1),
        "gate_t": gate_w.T,
        "select": select,
        "ident": np.eye(P, dtype=np.float32),
        "rank_key": rank_key,
    }
    arrays = {k: np.ascontiguousarray(a) for k, a in arrays.items()}
    nc = bacc.Bacc("TRN2", target_bir_lowering=False, num_devices=1)
    ins = {k: nc.dram_tensor(k, a.shape, mybir.dt.from_np(a.dtype), kind="ExternalInput").ap() for k, a in arrays.items()}
    out = nc.dram_tensor("out", arrays["x"].shape, F32, kind="ExternalOutput").ap()
    mixer_moe_kernel(nc, out=out, **ins)
    r = run_bass_kernel_spmd(nc, [arrays], core_ids=[0])
    return r.results[0]["out"]
```

```python
from contextlib import ExitStack

import concourse.bass as bass
from concourse import mybir

ALU = mybir.AluOpType
ACT = mybir.ActivationFunctionType
AX_X = mybir.AxisListType.X
F32 = mybir.dt.float32
F32R = mybir.dt.float32r

P = 128
GROUP = 512
TILES = GROUP // P
LN_EPS = 1e-5
CLIP_MIN = 1e-4
A_MIN = 1e-4
PRE_MAX = 20.0
LOWEST = -3.0e38
GATE_STEPS = 15
RSTD_STEPS = 6
MARGIN_STEP = 8
WARM_UP = 12


class Stage:

    def __init__(self, sem, per, base=0):
        self.sem, self.per, self.base = sem, per, base

    def at(self, window, done):
        return window * self.per + (self.base + done)


def mixer_moe_kernel(nc, x, first, late, w12_t, w3_t, first_at, late_at, out):
    BATCHES, L, D = x.shape
    GROUPS = L // GROUP
    EXPERTS, H2 = w12_t.shape[1:]
    HB = H2 // 2 // P
    UNITS = EXPERTS
    HALVES = HB
    DSTATE = (late_at["wx_bc"][2] - late_at["wx_bc"][1]) // 2
    INNER = late_at["b_dt"][0]
    NJ = DSTATE * INNER // P
    assert D == P and 2 * INNER == P and GROUPS == 2 and HB == 2

    x_v = x.rearrange("b (g t p) d -> b g p t d", g=GROUPS, p=P)
    out_v = out.rearrange("b (g t p) d -> b g p t d", g=GROUPS, p=P)

    with ExitStack() as ctx:
        def sb(name, shape, dt=F32):
            return ctx.enter_context(nc.sbuf_tensor(name, shape, dt))

        def stage(name, per, base=0):
            return Stage(ctx.enter_context(nc.semaphore(name)), per, base)

        def event(name):
            return ctx.enter_context(nc.semaphore(name))

        w12_f = sb("w12_f", [P, EXPERTS, H2])
        w12_hi = sb("w12_hi", [P, EXPERTS, H2], F32R)
        w12_lo = sb("w12_lo", [P, EXPERTS, H2], F32R)
        w3_sb = sb("w3_sb", [P, EXPERTS, HB, D])
        first_sb = sb("first_sb", [P, first.shape[1]])
        late_sb = sb("late_sb", [P, late.shape[1]])

        def part_of(tensor, where):
            rows, start, end = where
            return tensor[0:rows, start:end]

        id_sb, win_f, gate_f, a_in, key_flat = (part_of(first_sb, first_at[n]) for n in ("ident", "w_in", "gate", "a_log", "rank_key"))
        key_sb = key_flat.rearrange("p (t e) -> p t e", e=EXPERTS)
        taps, w_out_sb, wx_bc_sb, b_dt_sb, d_sb, wx_dt_sb, w_dt_sb = (
            part_of(late_sb, late_at[n]) for n in ("taps", "w_out", "wx_bc", "b_dt", "d_skip", "wx_dt", "w_dt"))
        win_hi = sb("win_hi", [P, P], F32R)
        win_lo = sb("win_lo", [P, P], F32R)
        gate_parts = sb("gate_parts", [P, 2 * EXPERTS], F32R)
        gate_hi, gate_lo = gate_parts[:, 0:EXPERTS], gate_parts[:, EXPERTS:2 * EXPERTS]
        wp = sb("wp", [P, P])
        wp_hi = sb("wp_hi", [P, P], F32R)
        wp_lo = sb("wp_lo", [INNER, P], F32R)
        a_abs = sb("a_abs", [P, NJ])
        a_exp = sb("a_exp", [P, NJ])
        a_ln = sb("a_ln", [P, NJ])
        a_sum = sb("a_sum", [P, NJ])
        a_neg = sb("a_neg", [P, NJ])
        power = sb("power", [P, TILES])
        quarter = sb("quarter", [P, TILES])

        WINDOWS = BATCHES * GROUPS
        x_sb = sb("x_sb", [P, WINDOWS, TILES, D])
        xt_hi = [sb(f"xt_hi{s}", [P, GROUP], F32R) for s in range(2)]
        xt_lo = [sb(f"xt_lo{s}", [P, GROUP], F32R) for s in range(2)]
        new_hi = sb("new_hi", [P, GROUP], F32R)
        new_lo = sb("new_lo", [P, GROUP], F32R)
        gates = [sb(f"gates{s}", [P, TILES, EXPERTS]) for s in range(2)]
        h_in = [sb(f"h_in{s}", [P, GROUP + 2]) for s in range(2)]

        bn = sb("bn", [P, 2 * TILES, 6])
        first_var_eps = sb("first_var_eps", [P, 2 * TILES])
        mean_var = sb("mean_var", [P, 2 * TILES, 2])
        mean_sum = sb("mean_sum", [P, TILES])
        mean_gap = sb("mean_gap", [P, TILES])
        gap_sq = sb("gap_sq", [P, TILES])
        square_sum = sb("square_sum", [P, TILES])
        neg_mean = sb("neg_mean", [P, TILES])
        shift = sb("shift", [P, 2 * TILES])
        var_eps = sb("var_eps", [P, TILES])
        rstd = sb("rstd", [P, 2 * TILES])
        xn = sb("xn", [P, TILES, D])
        xn_second = sb("xn_second", [P, TILES, D])
        low_score = sb("low_score", [P, 2 * TILES, EXPERTS])
        score = sb("score", [P, 2 * TILES, EXPERTS])
        score2 = sb("score2", [P, 2 * TILES, EXPERTS])
        top = [sb(f"top{n}", [P, 2 * TILES]) for n in range(2)]
        hit = [sb(f"hit{n}", [P, 2 * TILES, EXPERTS]) for n in range(2)]
        keyed = [sb(f"keyed{n}", [P, 2 * TILES, EXPERTS]) for n in range(2)]
        key_max = [sb(f"key_max{n}", [P, 2 * TILES]) for n in range(2)]
        one_hot = [sb(f"one_hot{n}", [P, 2 * TILES, EXPERTS]) for n in range(2)]
        margin = sb("margin", [P, 2 * TILES])
        lean = sb("lean", [P, 2 * TILES])
        both = sb("both", [P, 2 * TILES, EXPERTS])
        apart = sb("apart", [P, 2 * TILES, EXPERTS])
        leaned = sb("leaned", [P, 2 * TILES, EXPERTS])

        acc = [sb(f"acc{s}", [P, TILES, D]) for s in range(2)]

        g_sb = [sb(f"g_sb{a}", [P, GROUP]) for a in range(2)]
        hid = [[sb(f"hid{s}{a}", [P, GROUP]) for a in range(HALVES)] for s in range(2)]
        gated = [sb(f"gated{s}", [P, TILES, D]) for s in range(2)]

        conv = sb("conv", [P, GROUP])
        xx = [sb(f"xx{s}", [P, GROUP]) for s in range(2)]
        xz = sb("xz", [P, GROUP])
        x_parts = sb("x_parts", [P, GROUP], F32R)
        half_sum = [sb(f"half_sum{s}", [INNER, GROUP]) for s in range(2)]
        fold = sb("fold", [INNER, GROUP])
        bc = sb("bc", [P, GROUP])
        bc_dram = nc.dram_tensor("bc_dram", [2 * DSTATE, GROUP], F32, kind="Internal").ap()
        pre = sb("pre", [INNER, GROUP])
        pre_exp = sb("pre_exp", [INNER, GROUP])
        delta = sb("delta", [P, GROUP])
        decay = [sb(f"decay{j}", [P, GROUP]) for j in range(NJ)]
        bx_all = sb("bx_all", [P, NJ, GROUP])
        c_all = sb("c_all", [P, NJ, GROUP])
        bx = [bx_all[:, j, :] for j in range(NJ)]
        state = [[sb(f"state{s}{j}", [P, GROUP]) for j in range(NJ)] for s in range(2)]
        mix = sb("mix", [P, TILES, D])

        h_ps = [ctx.enter_context(nc.psum_tensor(f"h_ps{a}", [P, 2, GROUP], F32)) for a in range(2)]
        y_ps = [ctx.enter_context(nc.psum_tensor(f"y_ps{s}", [P, TILES, D], F32)) for s in range(2)]
        s_ps = [ctx.enter_context(nc.psum_tensor(f"s_ps{s}", [P, GROUP], F32)) for s in range(2)]

        small_loaded = event("small_loaded")
        late_loaded = event("late_loaded")
        w12_loaded = [event(f"w12_loaded{e}") for e in range(EXPERTS)]
        w3_loaded = [event(f"w3_loaded{e}") for e in range(EXPERTS)]
        xt_moved = [event(f"xt_moved{s}") for s in range(2)]
        x_loaded = [event(f"x_loaded{s}") for s in range(4)]
        consts_set = event("consts_set")
        win_hi_done = event("win_hi_done")
        win_lo_done = event("win_lo_done")
        w12_hi_done = event("w12_hi_done")
        w12_first_lo_done = event("w12_first_lo_done")
        w12_lo_done = event("w12_lo_done")
        a_dve_step = event("a_dve_step")
        a_act_step = event("a_act_step")
        w_comb_full = event("w_comb_full")
        wp_copied = event("wp_copied")
        wp_done = event("wp_done")
        wp_hi_done = event("wp_hi_done")
        wp_lo_done = event("wp_lo_done")
        bn_done = stage("bn_done", TILES, 2 * TILES)
        rstd_step = stage("rstd_step", RSTD_STEPS)
        xn_done = stage("xn_done", TILES, TILES)
        first_stats_step = event("first_stats_step")
        first_rstd_done = event("first_rstd_done")
        first_shift_done = event("first_shift_done")
        xn_first = [event(f"xn_first{s}") for s in range(2)]
        xt_full = stage("xt_full", 1, 2)
        xt_hi_done = stage("xt_hi_done", 1, 2)
        xt_lo_done = stage("xt_lo_done", 1, 2)
        score_full = stage("score_full", 1, 2)
        h_in_full = stage("h_in_full", 1, 2)
        h_in_done = stage("h_in_done", 1, 2)
        low_score_done = stage("low_score_done", 1, 2)
        score_kept = stage("score_kept", 1, 2)
        gate_stepped = stage("gate_stepped", GATE_STEPS, 2 * GATE_STEPS)
        lean_done = stage("lean_done", 1, 2)
        h_full = stage("h_full", UNITS * HALVES, 2)
        silu_done = stage("silu_done", UNITS * HALVES)
        hid_done = stage("hid_done", UNITS * HALVES, 2)
        y_full = stage("y_full", UNITS, 2)
        gated_done = stage("gated_done", UNITS, 2)
        acc_done = stage("acc_done", UNITS + 1, 3)
        acc_loaded = [event(f"acc_loaded{s}") for s in range(2)]
        out_stored = [event(f"out_stored{s}") for s in range(2)]
        conv_stepped = stage("conv_stepped", 3, 3)
        xz_done = stage("xz_done", 3)
        x_split = stage("x_split", 2)
        fold_done = stage("fold_done", 1, 1)
        y_done = stage("y_done", 1)
        proj_full = stage("proj_full", 1)
        bc_tanh_done = stage("bc_tanh_done", 1)
        pre_done = stage("pre_done", 1)
        bc_stored = stage("bc_stored", 16)
        b_spread = [stage(f"b_spread{k}", 32) for k in range(2)]
        c_spread = [stage(f"c_spread{k}", 32, 32) for k in range(2)]
        softplus_step = stage("softplus_step", 2)
        delta_done = stage("delta_done", 1)
        decay_done = stage("decay_done", NJ)
        clip_done = stage("clip_done", NJ)
        bx_done = stage("bx_done", NJ)
        drive_done = stage("drive_done", NJ)
        scan_done = stage("scan_done", NJ)
        c_state_done = stage("c_state_done", NJ, NJ)
        state_sum_step = stage("state_sum_step", NJ - 1)
        mix_full = stage("mix_full", 1)
        mix_done = stage("mix_done", 1, 1)

        block = ctx.enter_context(nc.Block())

        USES = ["proj", "xt", "h_in", "score", "mix"]

        def bank(g, use):
            return s_ps[(g * len(USES) + USES.index(use)) % 2]

        def flat(t):
            return t[:, :, :].rearrange("p t d -> p (t d)")

        first_scores_ps = flat(y_ps[0])
        comb_ps = flat(y_ps[1])

        @block.sync
        def _(sp):
            def load_expert(e):
                sp.dma_start(w12_f[:, e, :], w12_t[:, e, :]).then_inc(w12_loaded[e], 16)
                sp.dma_start(w3_sb[:, e, :, :], w3_t[:, e, :, :]).then_inc(w3_loaded[e], 16)

            def spread(row, to, done):
                rows = bc_dram[row:row + DSTATE, :].rearrange("(j m) t -> m j t", m=2)
                for k in range(2):
                    tiles = slice(k * NJ // 2, (k + 1) * NJ // 2)
                    for m in range(2):
                        sp.dma_start(to[m * INNER:(m + 1) * INNER, tiles, :],
                                     rows[m:m + 1, tiles].to_broadcast([INNER, NJ // 2, GROUP])).then_inc(done[k].sem, 16)

            def load_x(n, loaded):
                sp.dma_start(x_sb[:, n, :, :], x_v[n // GROUPS, n % GROUPS]).then_inc(loaded, 16)

            load_x(0, x_loaded[0])
            sp.dma_start(first_sb[:, :], first).then_inc(small_loaded, 16)
            load_x(1, x_loaded[1])
            load_expert(0)
            sp.dma_start(late_sb[:, :], late).then_inc(late_loaded, 16)
            load_expert(1)
            load_x(2, x_loaded[2])
            for e in range(2, EXPERTS):
                load_expert(e)
            for n in range(3, WINDOWS):
                load_x(n, x_loaded[3])

            def sequence(i, final=False):
                for g in range(GROUPS):
                    w = i * GROUPS + g
                    sp.wait_ge(x_loaded[g], 16)
                    sp.wait_ge(out_stored[g], 16 * i + 16)
                    sp.dma_start(acc[g][:, :, :], x_sb[:, w, :, :]).then_inc(acc_loaded[g], 16)
                    if g == 1:
                        sp.wait_ge(x_loaded[2], 16)
                        sp.wait_ge(x_loaded[3], 16 * (WINDOWS - 3))
                    if not final or g == 0:
                        sp.wait_ge(xt_lo_done.sem, xt_lo_done.at(w - 1, 1))
                        sp.wait_ge(h_full.sem, h_full.at(w, 0))
                        sp.dma_start(xt_hi[1 - g][:, :].bitcast(F32), new_hi[:, :].bitcast(F32)).then_inc(xt_moved[1 - g], 16)
                        sp.dma_start(xt_lo[1 - g][:, :].bitcast(F32), new_lo[:, :].bitcast(F32)).then_inc(xt_moved[1 - g], 16)
                    sp.wait_ge(bc_tanh_done.sem, bc_tanh_done.at(w, 1))
                    sp.wait_ge(c_spread[1].sem, c_spread[1].at(w - 1, 32))
                    sp.dma_start(bc_dram, bc[INNER:INNER + 2 * DSTATE, :]).then_inc(bc_stored.sem, 16)
                    sp.wait_ge(bc_stored.sem, bc_stored.at(w, 16))
                    sp.wait_ge(fold_done.sem, fold_done.at(w - 1, 1))
                    spread(0, bx_all, b_spread)
                    sp.wait_ge(c_state_done.sem, c_state_done.at(w - 1, NJ))
                    spread(DSTATE, c_all, c_spread)
                    sp.wait_ge(acc_done.sem, acc_done.at(w, UNITS + 1))
                    sp.dma_start(out_v[i, g], acc[g][:, :, :]).then_inc(out_stored[g], 16)

            with sp.Fori(0, BATCHES - 1) as i:
                sequence(i)
            sequence(BATCHES - 1, final=True)
            for g in range(GROUPS):
                sp.wait_ge(out_stored[g], 16 * (BATCHES + 1))
            sp.wait_ge(xt_moved[0], 32 * BATCHES)
            sp.wait_ge(xt_moved[1], 32 * BATCHES)

        @block.gpsimd
        def _(pool):
            for st in (xn_done, h_full, hid_done, y_full, gated_done, acc_done, c_state_done, fold_done, mix_done) + tuple(c_spread):
                pool.sem_inc(st.sem, st.base)
            for s in range(2):
                pool.sem_inc(out_stored[s], 16)
            pool.sem_inc(xt_moved[0], 32)
            nc.gpsimd.memset(wp[:, :], 0.0).then_inc(consts_set, 1)
            nc.gpsimd.memset(power[:, :], -0.5).then_inc(consts_set, 1)
            nc.gpsimd.memset(quarter[:, :], 0.25).then_inc(consts_set, 1)
            nc.gpsimd.memset(h_in[0][:, 0:1], 0.0).then_inc(consts_set, 1)
            nc.gpsimd.memset(h_in[1][:, GROUP + 1:GROUP + 2], 0.0).then_inc(consts_set, 1)
            pool.wait_ge(consts_set, 5)

            def inverse_deviation(w):
                n = slice(0, TILES)
                even, odd = bn[:, n, 0:3], bn[:, n, 3:6]
                pool.wait_ge(bn_done.sem, bn_done.at(w, TILES))
                nc.gpsimd.tensor_tensor(mean_sum[:, :], even[:, :, 1], odd[:, :, 1], ALU.add)
                nc.gpsimd.tensor_tensor(mean_gap[:, :], even[:, :, 1], odd[:, :, 1], ALU.subtract)
                nc.gpsimd.tensor_tensor(square_sum[:, :], even[:, :, 2], odd[:, :, 2], ALU.add).then_inc(rstd_step.sem, 1)
                pool.wait_ge(rstd_step.sem, rstd_step.at(w, 1))
                nc.gpsimd.tensor_tensor(gap_sq[:, :], mean_gap[:, :], mean_gap[:, :], ALU.mult)
                nc.gpsimd.tensor_scalar(neg_mean[:, :], mean_sum[:, :], -0.5, 0.0, ALU.mult, ALU.add)
                nc.gpsimd.tensor_scalar(square_sum[:, :], square_sum[:, :], 1.0 / D, LN_EPS, ALU.mult, ALU.add).then_inc(rstd_step.sem, 1)
                pool.wait_ge(rstd_step.sem, rstd_step.at(w, 2))
                nc.gpsimd.tensor_tensor(gap_sq[:, :], gap_sq[:, :], quarter[:, :], ALU.mult).then_inc(rstd_step.sem, 1)
                pool.wait_ge(rstd_step.sem, rstd_step.at(w, 3))
                nc.gpsimd.tensor_tensor(var_eps[:, :], square_sum[:, :], gap_sq[:, :], ALU.add).then_inc(rstd_step.sem, 1)
                pool.wait_ge(xn_done.sem, xn_done.at(w - 1, TILES))
                pool.wait_ge(rstd_step.sem, rstd_step.at(w, 4))
                nc.gpsimd.tensor_tensor(rstd[:, n], var_eps[:, :], power[:, :], ALU.pow).then_inc(rstd_step.sem, 1)
                pool.wait_ge(rstd_step.sem, rstd_step.at(w, 5))
                nc.gpsimd.tensor_tensor(shift[:, n], neg_mean[:, :], rstd[:, n], ALU.mult).then_inc(rstd_step.sem, 1)

            pool.wait_ge(first_stats_step, 2)
            for s in range(2):
                n = slice(s * TILES, (s + 1) * TILES)
                nc.gpsimd.tensor_tensor(rstd[:, n], first_var_eps[:, n], power[:, :], ALU.pow).then_inc(first_rstd_done, 1)
            pool.wait_ge(late_loaded, 16)
            nc.gpsimd.tensor_copy(wp[:, INNER:INNER + 2 * DSTATE], wx_bc_sb).then_inc(wp_copied, 1)
            for e in range(1, EXPERTS):
                pool.wait_ge(w12_hi_done, e + 1)
                nc.gpsimd.tensor_tensor(w12_lo[:, e, :], w12_f[:, e, :], w12_hi[:, e, :].bitcast(F32), ALU.subtract).then_inc(w12_lo_done, 1)
            for s in range(2):
                pool.wait_ge(xn_first[s], TILES)

            def sequence(i, final=False):
                for g in range(GROUPS):
                    w = i * GROUPS + g

                    def add_expert(u):
                        pool.wait_ge(gated_done.sem, gated_done.at(w, u + 1))
                        if u > 0:
                            pool.wait_ge(acc_done.sem, acc_done.at(w, u + u // (UNITS - 1)))
                        else:
                            pool.wait_ge(acc_loaded[g], 16 * i + 16)
                        nc.gpsimd.tensor_tensor(flat(acc[g]), flat(acc[g]), flat(gated[u % 2]),
                                                ALU.add).then_inc(acc_done.sem, 1)

                    def add_tile(j):
                        pool.wait_ge(c_state_done.sem, c_state_done.at(w, j + 1))
                        if j > 1:
                            pool.wait_ge(state_sum_step.sem, state_sum_step.at(w, j - 1))
                        if j < NJ - 1:
                            nc.gpsimd.tensor_tensor(bx[0][:, :], bx[0][:, :], bx[j][:, :], ALU.add).then_inc(state_sum_step.sem, 1)
                        else:
                            for s in range(2):
                                rows = slice(s * INNER, (s + 1) * INNER)
                                last = nc.gpsimd.tensor_tensor(half_sum[s][:, :], bx[0][rows, :], bx[j][rows, :], ALU.add)
                            last.then_inc(state_sum_step.sem, 1)

                    def fold_states():
                        pool.wait_ge(state_sum_step.sem, state_sum_step.at(w, NJ - 1))
                        nc.gpsimd.tensor_tensor(fold[:, :], half_sum[0][:, :], half_sum[1][:, :], ALU.add).then_inc(fold_done.sem, 1)

                    def add_mix():
                        pool.wait_ge(mix_done.sem, mix_done.at(w, 1))
                        pool.wait_ge(acc_done.sem, acc_done.at(w, UNITS - 1))
                        nc.gpsimd.tensor_tensor(flat(acc[g]), flat(acc[g]), flat(mix), ALU.add).then_inc(acc_done.sem, 1)

                    if not final:
                        inverse_deviation(w)
                    add_expert(0)
                    add_expert(1)
                    add_expert(2)
                    add_expert(3)
                    add_tile(1)
                    add_tile(2)
                    add_tile(3)
                    fold_states()
                    add_expert(4)
                    add_expert(5)
                    add_expert(6)
                    add_mix()
                    add_expert(7)

            with pool.Fori(0, BATCHES - 1) as i:
                sequence(i)
            sequence(BATCHES - 1, final=True)

        @block.scalar
        def _(act):
            def keep_xt_hi(w, hi, ps):
                act.wait_ge(xt_full.sem, xt_full.at(w, 1))
                nc.scalar.copy(hi[:, :], ps[:, :]).then_inc(xt_hi_done.sem, 1)

            def normalise(w, x_ap, t):
                if t == 0:
                    act.wait_ge(rstd_step.sem, rstd_step.at(w, RSTD_STEPS))
                nc.scalar.activation(xn[:, t, :], x_ap[:, t, :], ACT.Identity, bias=shift[:, t:t + 1],
                                     scale=rstd[:, t:t + 1]).then_inc(xn_done.sem, 1)

            def keep_h_in(w, slot, ps, halo):
                act.wait_ge(h_in_full.sem, h_in_full.at(w, 1))
                last = nc.scalar.copy(h_in[slot][:, 1:GROUP + 1], ps[:, :])
                if halo:
                    nc.scalar.copy(h_in[0][:, GROUP + 1:GROUP + 2], ps[:, 0:1])
                    act.wait_ge(h_in_done.sem, h_in_done.at(w - 1, 1))
                    last = nc.scalar.copy(h_in[1][:, 0:1], h_in[0][:, GROUP:GROUP + 1])
                last.then_inc(h_in_done.sem, 1)

            def first_tap(w, slot, first=False):
                if not first:
                    act.wait_ge(xz_done.sem, xz_done.at(w, 3))
                act.wait_ge(h_in_done.sem, h_in_done.at(w if slot == 0 else w - 1, 1))
                nc.scalar.activation(conv[:, :], h_in[slot][:, 0:GROUP], ACT.Copy, scale=taps[:, 0:1]).then_inc(conv_stepped.sem, 1)

            def lean_to_best(w, tiles=TILES):
                windows = tiles // TILES
                act.wait_ge(gate_stepped.sem, 2 * MARGIN_STEP if windows == 2 else gate_stepped.at(w, MARGIN_STEP))
                nc.scalar.activation(lean[:, 0:tiles], margin[:, 0:tiles], ACT.Tanh, scale=0.5).then_inc(lean_done.sem, windows)

            def round_w12(e):
                act.wait_ge(w12_loaded[e], 16)
                nc.scalar.copy(w12_hi[:, e, :], w12_f[:, e, :]).then_inc(w12_hi_done, 1)

            nc.scalar.preload_act_table_set("natural_log_exp_and_others")
            act.wait_ge(a_dve_step, 1)
            nc.scalar.activation(a_exp[:, :], a_abs[:, :], ACT.Exp, scale=-1.0).then_inc(a_act_step, 1)
            act.wait_ge(a_act_step, 1)
            nc.scalar.activation(a_ln[:, :], a_exp[:, :], ACT.Ln, bias=1.0).then_inc(a_act_step, 1)
            nc.scalar.preload_act_table_set("silu_and_others")
            act.wait_ge(small_loaded, 16)
            nc.scalar.copy(win_hi[:, :], win_f[:, :])
            nc.scalar.copy(gate_hi, gate_f).then_inc(win_hi_done, 1)
            for s, xn_of in enumerate((xn, xn_second)):
                act.wait_ge(first_shift_done, s + 1)
                for t in range(TILES // 2, TILES):
                    n = slice(s * TILES + t, s * TILES + t + 1)
                    nc.scalar.activation(xn_of[:, t, :], x_sb[:, s, t, :], ACT.Identity, bias=shift[:, n],
                                         scale=rstd[:, n]).then_inc(xn_first[s], 1)
            keep_xt_hi(-2, xt_hi[0], s_ps[0])
            round_w12(0)
            keep_xt_hi(-1, new_hi, s_ps[1])
            act.wait_ge(w_comb_full, 1)
            for rows in (0, INNER):
                last = nc.scalar.copy(wp[rows:rows + INNER, 0:INNER], comb_ps[0:INNER, 0:INNER])
            last.then_inc(wp_done, 1)
            act.wait_ge(wp_done, 1)
            act.wait_ge(wp_copied, 1)
            nc.scalar.copy(wp_hi[:, :], wp[:, :]).then_inc(wp_hi_done, 1)
            for e in range(1, 4):
                round_w12(e)
            keep_h_in(-2, 0, s_ps[0], False)
            keep_h_in(-1, 1, s_ps[1], True)
            first_tap(-1, 0, True)
            round_w12(4)
            lean_to_best(-2, 2 * TILES)
            for e in range(5, EXPERTS):
                round_w12(e)

            def sequence(i, final=False):
                for g in range(GROUPS):
                    w = i * GROUPS + g
                    new = w + GROUPS

                    def keep_mix():
                        act.wait_ge(mix_full.sem, mix_full.at(w, 1))
                        nc.scalar.copy(flat(mix), bank(g, "mix")[:, :]).then_inc(mix_done.sem, 1)

                    def silu(u, a):
                        act.wait_ge(h_full.sem, h_full.at(w, HALVES * u + a + 1))
                        nc.scalar.activation(g_sb[a][:, :], h_ps[a][:, 0, :], ACT.Silu).then_inc(silu_done.sem, 1)

                    def conv_silu(part):
                        if part == 0:
                            act.wait_ge(conv_stepped.sem, conv_stepped.at(w - 1, 3))
                        to = (xx[g][0:INNER, :], xx[g][INNER:P, :], xz[INNER:P, :])[part]
                        from_ = conv[INNER:P, :] if part == 2 else conv[0:INNER, :]
                        nc.scalar.activation(to, from_, ACT.Silu).then_inc(xz_done.sem, 1)

                    def round_x():
                        act.wait_ge(xz_done.sem, xz_done.at(w, 2))
                        nc.scalar.copy(x_parts[:, :], xx[g][:, :]).then_inc(x_split.sem, 1)

                    def bc_tanh():
                        act.wait_ge(proj_full.sem, proj_full.at(w, 1))
                        rows = slice(INNER, INNER + 2 * DSTATE)
                        nc.scalar.activation(bc[rows, :], bank(g, "proj")[rows, :], ACT.Tanh).then_inc(bc_tanh_done.sem, 1)

                    def softplus_exp():
                        act.wait_ge(pre_done.sem, pre_done.at(w, 1))
                        nc.scalar.activation(pre_exp[:, :], pre[:, :], ACT.Exp).then_inc(softplus_step.sem, 1)

                    def softplus_ln():
                        act.wait_ge(softplus_step.sem, softplus_step.at(w, 1))
                        nc.scalar.activation(pre_exp[:, :], pre_exp[:, :], ACT.Ln, bias=1.0).then_inc(softplus_step.sem, 1)

                    def decay_exp(j):
                        if j == 0:
                            act.wait_ge(delta_done.sem, delta_done.at(w, 1))
                        nc.scalar.activation(decay[j][:, :], delta[:, :], ACT.Exp, scale=a_neg[:, j:j + 1]).then_inc(decay_done.sem, 1)

                    def keep_xt_hi_of_next():
                        act.wait_ge(xt_moved[1 - g], 32 * (i + 1 + g))
                        keep_xt_hi(w, new_hi, bank(g, "xt"))

                    silu(0, 0)
                    conv_silu(0)
                    silu(0, 1)
                    conv_silu(1)
                    round_x()
                    silu(1, 0)
                    silu(1, 1)
                    bc_tanh()
                    if not final:
                        normalise(w, x_sb[:, new], 0)
                        normalise(w, x_sb[:, new], 1)
                        normalise(w, x_sb[:, new], 2)
                    silu(2, 0)
                    silu(2, 1)
                    nc.scalar.preload_act_table_set("natural_log_exp_and_others")
                    softplus_exp()
                    if not final:
                        normalise(w, x_sb[:, new], 3)
                    softplus_ln()
                    if not final:
                        keep_xt_hi_of_next()
                    decay_exp(0)
                    decay_exp(1)
                    decay_exp(2)
                    decay_exp(3)
                    nc.scalar.preload_act_table_set("silu_and_others")
                    silu(3, 0)
                    silu(3, 1)
                    silu(4, 0)
                    conv_silu(2)
                    silu(4, 1)
                    if not final:
                        keep_h_in(w, g, bank(g, "h_in"), g == 1)
                    silu(5, 0)
                    silu(5, 1)
                    silu(6, 0)
                    silu(6, 1)
                    if not final or g == 0:
                        first_tap(w, 1 - g)
                    silu(7, 0)
                    silu(7, 1)
                    if not final:
                        lean_to_best(w)
                    keep_mix()

            with act.Fori(0, BATCHES - 1) as i:
                sequence(i)
            sequence(BATCHES - 1, final=True)

        @block.vector
        def _(dve):
            def statistics(x_ap, tile=0):
                for t in range(TILES):
                    nc.vector.bn_stats(bn[:, tile + t, :], x_ap[:, t, :]).then_inc(bn_done.sem, 1)

            def keep_xt_lo(w, hi, lo, ps):
                dve.wait_ge(xt_hi_done.sem, xt_hi_done.at(w, 1))
                nc.vector.tensor_tensor(lo[:, :], ps[:, :], hi[:, :].bitcast(F32), ALU.subtract).then_inc(xt_lo_done.sem, 1)

            def wide(t, n):
                return t[:, n].unsqueeze(2).to_broadcast([P, n.stop, EXPERTS])

            def keep_scores(w, ps, tiles=TILES):
                parts = ps[:, 0:tiles * 2 * EXPERTS].rearrange("p (t k e) -> p t k e", k=2, e=EXPERTS)
                dve.wait_ge(score_full.sem, score_full.at(w, tiles // TILES))
                nc.vector.tensor_copy(low_score[:, 0:tiles, :], parts[:, :, 1, :]).then_inc(low_score_done.sem, tiles // TILES)
                dve.wait_ge(low_score_done.sem, low_score_done.at(w, tiles // TILES))
                nc.vector.tensor_tensor(score[:, 0:tiles, :], parts[:, :, 0, :], low_score[:, 0:tiles, :], ALU.add).then_inc(score_kept.sem, tiles // TILES)

            def next_tap(w, slot, k):
                dve.wait_ge(conv_stepped.sem, conv_stepped.at(w, k))
                nc.vector.scalar_tensor_tensor(out=conv[:, :], in0=h_in[slot][:, k:k + GROUP], scalar=taps[:, k:k + 1],
                                               in1=conv[:, :], op0=ALU.mult, op1=ALU.add).then_inc(conv_stepped.sem, 1)

            def gate_step(w, slots, n):
                windows = len(slots)
                tiles = slice(0, windows * TILES)

                def stepped(k):
                    return 2 * k if windows == 2 else gate_stepped.at(w, k)

                if n == 1:
                    dve.wait_ge(score_kept.sem, score_kept.at(w, windows))
                else:
                    dve.wait_ge(gate_stepped.sem, stepped(n - 1))
                k, from_, m = (0, score, n - 1) if n < 6 else (1, score2, n - 7 if n < 9 else n - 8)
                if n == 6:
                    last = nc.vector.scalar_tensor_tensor(out=score2[:, tiles, :], in0=one_hot[0][:, tiles, :], scalar=LOWEST,
                                                          in1=score[:, tiles, :], op0=ALU.mult, op1=ALU.add)
                elif n == MARGIN_STEP:
                    last = nc.vector.tensor_tensor(margin[:, tiles], top[0][:, tiles], top[1][:, tiles], ALU.subtract)
                elif n == 13:
                    nc.vector.tensor_tensor(both[:, tiles, :], one_hot[0][:, tiles, :], one_hot[1][:, tiles, :], ALU.add)
                    last = nc.vector.tensor_tensor(apart[:, tiles, :], one_hot[0][:, tiles, :], one_hot[1][:, tiles, :], ALU.subtract)
                elif n == 14:
                    dve.wait_ge(lean_done.sem, lean_done.at(w, windows))
                    last = nc.vector.scalar_tensor_tensor(out=leaned[:, tiles, :], in0=apart[:, tiles, :], scalar=0.5,
                                                          in1=wide(lean, tiles), op0=ALU.mult, op1=ALU.mult)
                elif n == 15:
                    for s in slots:
                        own = slice((s if windows == 2 else 0) * TILES, (s if windows == 2 else 0) * TILES + TILES)
                        last = nc.vector.scalar_tensor_tensor(out=gates[s][:, :, :], in0=both[:, own, :], scalar=0.5,
                                                              in1=leaned[:, own, :], op0=ALU.mult, op1=ALU.add)
                elif m == 0:
                    last = nc.vector.tensor_reduce(top[k][:, tiles], from_[:, tiles, :], AX_X, ALU.max)
                elif m == 1:
                    last = nc.vector.tensor_tensor(hit[k][:, tiles, :], from_[:, tiles, :], wide(top[k], tiles), ALU.is_equal)
                elif m == 2:
                    keys = key_sb[:, 0:TILES, :] if windows == 1 else key_sb[:, :, :]
                    last = nc.vector.tensor_tensor(keyed[k][:, tiles, :], hit[k][:, tiles, :], keys, ALU.mult)
                elif m == 3:
                    last = nc.vector.tensor_reduce(key_max[k][:, tiles], keyed[k][:, tiles, :], AX_X, ALU.max)
                elif m == 4:
                    last = nc.vector.tensor_tensor(one_hot[k][:, tiles, :], keyed[k][:, tiles, :], wide(key_max[k], tiles), ALU.is_equal)
                last.then_inc(gate_stepped.sem, windows)

            dve.wait_ge(x_loaded[0], 16)
            statistics(x_sb[:, 0])
            dve.wait_ge(small_loaded, 16)
            nc.vector.scalar_tensor_tensor(out=a_abs[:, :], in0=a_in[:, :], scalar=-1.0, in1=a_in[:, :],
                                           op0=ALU.mult, op1=ALU.max).then_inc(a_dve_step, 1)
            dve.wait_ge(x_loaded[1], 16)
            statistics(x_sb[:, 1], TILES)
            dve.wait_ge(bn_done.sem, bn_done.at(-1, TILES))
            for t in range(2 * TILES):
                last = nc.vector.bn_aggr(mean_var[:, t, :], bn[:, t, :])
            last.then_inc(first_stats_step, 1)
            dve.wait_ge(first_stats_step, 1)
            nc.vector.tensor_scalar(first_var_eps[:, :], mean_var[:, :, 1], LN_EPS, None, ALU.add).then_inc(first_stats_step, 1)

            def first_shift(s):
                dve.wait_ge(first_rstd_done, s + 1)
                n = slice(s * TILES, (s + 1) * TILES)
                nc.vector.scalar_tensor_tensor(out=shift[:, n], in0=mean_var[:, n, 0], scalar=-1.0, in1=rstd[:, n],
                                               op0=ALU.mult, op1=ALU.mult).then_inc(first_shift_done, 1)

            first_shift(0)
            first_shift(1)
            for s, xn_of in enumerate((xn, xn_second)):
                dve.wait_ge(first_shift_done, s + 1)
                for t in range(TILES // 2):
                    n = slice(s * TILES + t, s * TILES + t + 1)
                    nc.vector.tensor_scalar(xn_of[:, t, :], x_sb[:, s, t, :], rstd[:, n], shift[:, n], ALU.mult, ALU.add).then_inc(xn_first[s], 1)
            dve.wait_ge(a_act_step, 2)
            nc.vector.scalar_tensor_tensor(out=a_sum[:, :], in0=a_in[:, :], scalar=0.0, in1=a_ln[:, :],
                                           op0=ALU.max, op1=ALU.add).then_inc(a_dve_step, 1)
            dve.wait_ge(a_dve_step, 2)
            nc.vector.tensor_scalar(a_neg[:, :], a_sum[:, :], A_MIN, -1.0, ALU.add, ALU.mult).then_inc(a_dve_step, 1)
            dve.wait_ge(win_hi_done, 1)
            nc.vector.tensor_tensor(win_lo[:, :], win_f[:, :], win_hi[:, :].bitcast(F32), ALU.subtract)
            nc.vector.tensor_tensor(gate_lo, gate_f, gate_hi.bitcast(F32), ALU.subtract).then_inc(win_lo_done, 1)
            keep_xt_lo(-2, xt_hi[0], xt_lo[0], s_ps[0])
            keep_xt_lo(-1, new_hi, new_lo, s_ps[1])
            dve.wait_ge(w12_hi_done, 1)
            nc.vector.tensor_tensor(w12_lo[:, 0, :], w12_f[:, 0, :], w12_hi[:, 0, :].bitcast(F32), ALU.subtract).then_inc(w12_first_lo_done, 1)
            dve.wait_ge(wp_hi_done, 1)
            nc.vector.tensor_tensor(wp_lo[:, :], wp[0:INNER, :], wp_hi[0:INNER, :].bitcast(F32), ALU.subtract).then_inc(wp_lo_done, 1)
            keep_scores(-2, first_scores_ps, 2 * TILES)
            for n in range(1, 9):
                gate_step(-2, (0, 1), n)
            next_tap(-1, 0, 1)
            for n in range(9, 11):
                gate_step(-2, (0, 1), n)
            next_tap(-1, 0, 2)
            for n in range(11, GATE_STEPS + 1):
                gate_step(-2, (0, 1), n)

            def sequence(i, final=False):
                for g in range(GROUPS):
                    w = i * GROUPS + g
                    new = w + GROUPS

                    def product(u, a):
                        dve.wait_ge(silu_done.sem, silu_done.at(w, HALVES * u + a + 1))
                        dve.wait_ge(y_full.sem, y_full.at(w, u - 1))
                        nc.vector.tensor_tensor(hid[u % 2][a][:, :], h_ps[a][:, 1, :], g_sb[a][:, :], ALU.mult).then_inc(hid_done.sem, 1)

                    def gate(u):
                        dve.wait_ge(y_full.sem, y_full.at(w, u + 1))
                        dve.wait_ge(acc_done.sem, acc_done.at(w, u - 1 if u else -2))
                        if u == 0:
                            dve.wait_ge(gate_stepped.sem, gate_stepped.at(w - 2, GATE_STEPS))
                        nc.vector.tensor_tensor(gated[u % 2][:, :, :], y_ps[u % 2][:, :, :],
                                                gates[g][:, :, u].unsqueeze(2).to_broadcast([P, TILES, D]), ALU.mult).then_inc(gated_done.sem, 1)

                    def split_x():
                        dve.wait_ge(x_split.sem, x_split.at(w, 1))
                        nc.vector.tensor_tensor(x_parts[INNER:P, :], xx[g][INNER:P, :], x_parts[INNER:P, :].bitcast(F32),
                                                ALU.subtract).then_inc(x_split.sem, 1)

                    def add_skip():
                        dve.wait_ge(fold_done.sem, fold_done.at(w, 1))
                        nc.vector.scalar_tensor_tensor(out=xz[0:INNER, :], in0=xx[g][0:INNER, :], scalar=d_sb[:, 0:1],
                                                       in1=fold[:, :], op0=ALU.mult, op1=ALU.subtract).then_inc(y_done.sem, 1)

                    def keep_pre():
                        dve.wait_ge(proj_full.sem, proj_full.at(w, 1))
                        nc.vector.tensor_scalar(pre[:, :], bank(g, "proj")[0:INNER, :], b_dt_sb[:, 0:1], PRE_MAX,
                                                ALU.add, ALU.min).then_inc(pre_done.sem, 1)

                    def b_times_x(j):
                        dve.wait_ge(b_spread[j * 2 // NJ].sem, b_spread[j * 2 // NJ].at(w, 32))
                        if j == 0:
                            dve.wait_ge(xz_done.sem, xz_done.at(w, 2))
                        nc.vector.tensor_tensor(bx[j][:, :], bx[j][:, :], xx[g][:, :], ALU.mult).then_inc(bx_done.sem, 1)

                    def clip_delta():
                        dve.wait_ge(softplus_step.sem, softplus_step.at(w, 2))
                        nc.vector.tensor_scalar(delta[0:INNER, :], pre_exp[:, :], CLIP_MIN, 1.0, ALU.max, ALU.min)
                        nc.vector.tensor_scalar(delta[INNER:P, :], pre_exp[:, :], CLIP_MIN, 1.0, ALU.max, ALU.min).then_inc(delta_done.sem, 1)

                    def negative_drive(j):
                        dve.wait_ge(clip_done.sem, clip_done.at(w, j + 1))
                        dve.wait_ge(bx_done.sem, bx_done.at(w, j + 1))
                        nc.vector.scalar_tensor_tensor(out=bx[j][:, :], in0=decay[j][:, :], scalar=1.0, in1=bx[j][:, :],
                                                       op0=ALU.subtract, op1=ALU.mult).then_inc(drive_done.sem, 1)

                    def scan(j):
                        dve.wait_ge(drive_done.sem, drive_done.at(w, j + 1))
                        first = 0.0 if g == 0 else state[0][j][:, GROUP - 1:GROUP]
                        nc.vector.tensor_tensor_scan(state[g][j][:, :], decay[j][:, :], bx[j][:, :], first, ALU.mult, ALU.add).then_inc(scan_done.sem, 1)

                    def c_times_state(j):
                        dve.wait_ge(c_spread[j * 2 // NJ].sem, c_spread[j * 2 // NJ].at(w, 32))
                        dve.wait_ge(scan_done.sem, scan_done.at(w, j + 1))
                        nc.vector.tensor_tensor(bx[j][:, :], c_all[:, j, :], state[g][j][:, :], ALU.mult).then_inc(c_state_done.sem, 1)

                    def new_gate(n):
                        if n == GATE_STEPS:
                            dve.wait_ge(gated_done.sem, gated_done.at(w, UNITS))
                        gate_step(w, (g,), n)

                    def statistics_of_next():
                        if g == 0:
                            dve.wait_ge(x_loaded[2], 16)
                        else:
                            dve.wait_ge(x_loaded[3], 16 * (WINDOWS - 3))
                        statistics(x_sb[:, new])

                    def clip_decay(j):
                        dve.wait_ge(decay_done.sem, decay_done.at(w, j + 1))
                        nc.vector.tensor_scalar(decay[j][:, :], decay[j][:, :], CLIP_MIN, 1.0, ALU.max, ALU.min).then_inc(clip_done.sem, 1)

                    product(0, 0)
                    if not final:
                        statistics_of_next()
                    product(0, 1)
                    split_x()
                    product(1, 0)
                    product(1, 1)
                    keep_pre()
                    product(2, 0)
                    product(2, 1)
                    gate(0)
                    clip_delta()
                    gate(1)
                    b_times_x(0)
                    if not final:
                        keep_xt_lo(w, new_hi, new_lo, bank(g, "xt"))
                    clip_decay(0)
                    clip_decay(1)
                    clip_decay(2)
                    negative_drive(0)
                    b_times_x(1)
                    scan(0)
                    product(3, 0)
                    product(3, 1)
                    negative_drive(1)
                    gate(2)
                    b_times_x(2)
                    product(4, 0)
                    b_times_x(3)
                    scan(1)
                    product(4, 1)
                    negative_drive(2)
                    gate(3)
                    scan(2)
                    c_times_state(0)
                    product(5, 0)
                    clip_decay(3)
                    product(5, 1)
                    c_times_state(1)
                    negative_drive(3)
                    c_times_state(2)
                    scan(3)
                    product(6, 0)
                    c_times_state(3)
                    if not final:
                        keep_scores(w, bank(g, "score"))
                    product(6, 1)
                    if not final:
                        new_gate(1)
                        new_gate(2)
                    gate(4)
                    if not final:
                        new_gate(3)
                    gate(5)
                    if not final:
                        new_gate(4)
                        new_gate(5)
                    product(7, 0)
                    if not final:
                        new_gate(6)
                    product(7, 1)
                    if not final:
                        new_gate(7)
                    if not final or g == 0:
                        next_tap(w, 1 - g, 1)
                    if not final:
                        new_gate(8)
                    add_skip()
                    if not final:
                        new_gate(9)
                    gate(6)
                    if not final:
                        new_gate(10)
                        new_gate(11)
                    gate(7)
                    if not final:
                        new_gate(12)
                    if not final or g == 0:
                        next_tap(w, 1 - g, 2)
                    if not final:
                        new_gate(13)
                        new_gate(14)
                        new_gate(15)

            with dve.Fori(0, BATCHES - 1) as i:
                sequence(i)
            sequence(BATCHES - 1, final=True)

        @block.tensor
        def _(pe):
            def transpose(xn, ps):
                for t in range(TILES):
                    last = nc.tensor.transpose(ps[:, t * P:(t + 1) * P], xn[:, t, :], id_sb[:, :])
                last.then_inc(xt_full.sem, 1)

            def three_pass(out_ps, left_hi, left_lo, right_hi, right_lo):
                nc.tensor.matmul(out_ps, left_lo, right_hi, start=True, stop=False)
                nc.tensor.matmul(out_ps, left_hi, right_lo, start=False, stop=False)
                return nc.tensor.matmul(out_ps, left_hi, right_hi, start=False, stop=True)

            def scores(w, hi, lo, ps):
                pe.wait_ge(xt_lo_done.sem, xt_lo_done.at(w, 1))
                for t in range(TILES):
                    c = slice(t * P, (t + 1) * P)
                    at = t * 2 * EXPERTS
                    nc.tensor.matmul(ps[:, at:at + 2 * EXPERTS], hi[:, c], gate_parts[:, :], start=True, stop=False)
                    last = nc.tensor.matmul(ps[:, at:at + EXPERTS], lo[:, c], gate_hi, start=False, stop=True)
                last.then_inc(score_full.sem, 1)

            def project_in(w, hi, lo, ps):
                pe.wait_ge(xt_lo_done.sem, xt_lo_done.at(w, 1))
                three_pass(ps[:, :], win_hi[:, :], win_lo[:, :], hi[:, :], lo[:, :]).then_inc(h_in_full.sem, 1)

            def keep_busy(products):
                for _ in range(products):
                    nc.tensor.matmul(h_ps[0][:, 0, 0:P], id_sb[:, :], win_f[:, :], start=True, stop=True)

            pe.wait_ge(small_loaded, 16)
            keep_busy(WARM_UP)
            pe.wait_ge(late_loaded, 16)
            nc.tensor.matmul(comb_ps[0:INNER, 0:INNER], wx_dt_sb[:, :], w_dt_sb[:, :], start=True, stop=True).then_inc(w_comb_full, 1)
            for s, xn_of in enumerate((xn, xn_second)):
                pe.wait_ge(xn_first[s], TILES)
                transpose(xn_of, s_ps[s])
                keep_busy(2 + 2 * s)
            pe.wait_ge(win_lo_done, 1)
            scores(-2, xt_hi[0], xt_lo[0], first_scores_ps)
            scores(-1, new_hi, new_lo, first_scores_ps[:, TILES * 2 * EXPERTS:])
            project_in(-2, xt_hi[0], xt_lo[0], s_ps[0])
            project_in(-1, new_hi, new_lo, s_ps[1])
            pe.wait_ge(wp_lo_done, 1)
            keep_busy(WARM_UP)

            def sequence(i, final=False):
                for g in range(GROUPS):
                    w = i * GROUPS + g

                    def hidden(u, a):
                        if g == 0 and a == 0:
                            pe.wait_ge(w12_lo_done if u else w12_first_lo_done, u or 1)
                        if u == 0 and a == 0:
                            pe.wait_ge(xt_moved[g], 32 * i + 32)
                        pe.wait_ge(hid_done.sem, hid_done.at(w, HALVES * u + a - 1))
                        for part in range(2):
                            c = slice((part * HALVES + a) * P, (part * HALVES + a + 1) * P)
                            last = three_pass(h_ps[a][:, part, :], w12_hi[:, u, c], w12_lo[:, u, c], xt_hi[g][:, :], xt_lo[g][:, :])
                        last.then_inc(h_full.sem, 1)

                    def expert_out(u):
                        if g == 0:
                            pe.wait_ge(w3_loaded[u], 16)
                        pe.wait_ge(hid_done.sem, hid_done.at(w, HALVES * (u + 1)))
                        pe.wait_ge(gated_done.sem, gated_done.at(w, u - 1))
                        for t in range(TILES):
                            for a in range(HALVES):
                                last = nc.tensor.matmul(y_ps[u % 2][:, t, :], hid[u % 2][a][:, t * P:(t + 1) * P], w3_sb[:, u, a, :],
                                                        start=(a == 0), stop=(a == HALVES - 1))
                        last.then_inc(y_full.sem, 1)

                    def transpose_xn():
                        pe.wait_ge(xn_done.sem, xn_done.at(w, TILES))
                        transpose(xn, bank(g, "xt"))

                    def project():
                        pe.wait_ge(x_split.sem, x_split.at(w, 2))
                        nc.tensor.matmul(bank(g, "proj")[:, :], wp_lo[:, :], x_parts[0:INNER, :], start=True, stop=False)
                        nc.tensor.matmul(bank(g, "proj")[:, :], wp_hi[:, :], x_parts[:, :], start=False, stop=True).then_inc(proj_full.sem, 1)

                    def project_out():
                        pe.wait_ge(xz_done.sem, xz_done.at(w, 3))
                        pe.wait_ge(y_done.sem, y_done.at(w, 1))
                        for t in range(TILES):
                            c = slice(t * P, (t + 1) * P)
                            last = nc.tensor.matmul(bank(g, "mix")[:, c], xz[:, c], w_out_sb[:, :], start=True, stop=True)
                        last.then_inc(mix_full.sem, 1)

                    hidden(0, 0)
                    hidden(0, 1)
                    hidden(1, 0)
                    hidden(1, 1)
                    if final and g == 1:
                        pe.wait_ge(mix_done.sem, mix_done.at(w - 2, 1))
                    else:
                        pe.wait_ge(score_kept.sem, score_kept.at(w - 1, 1))
                    project()
                    hidden(2, 0)
                    hidden(2, 1)
                    expert_out(0)
                    expert_out(1)
                    if not final:
                        pe.wait_ge(mix_done.sem, mix_done.at(w - 1, 1))
                        transpose_xn()
                    hidden(3, 0)
                    expert_out(2)
                    if not final:
                        pe.wait_ge(pre_done.sem, pre_done.at(w, 1))
                        pe.wait_ge(bc_tanh_done.sem, bc_tanh_done.at(w, 1))
                        project_in(w, new_hi, new_lo, bank(g, "h_in"))
                    hidden(3, 1)
                    if not final:
                        pe.wait_ge(xt_lo_done.sem, xt_lo_done.at(w, 1))
                        scores(w, new_hi, new_lo, bank(g, "score"))
                    hidden(4, 0)
                    hidden(4, 1)
                    expert_out(3)
                    hidden(5, 0)
                    hidden(5, 1)
                    expert_out(4)
                    hidden(6, 0)
                    hidden(6, 1)
                    expert_out(5)
                    hidden(7, 0)
                    hidden(7, 1)
                    expert_out(6)
                    expert_out(7)
                    if final:
                        pe.wait_ge(pre_done.sem, pre_done.at(w, 1))
                        pe.wait_ge(bc_tanh_done.sem, bc_tanh_done.at(w, 1))
                    else:
                        pe.wait_ge(h_in_done.sem, h_in_done.at(w, 1))
                    project_out()

            with pe.Fori(0, BATCHES - 1) as i:
                sequence(i)
            sequence(BATCHES - 1, final=True)


def kernel(**inputs):
    import numpy as np
    import concourse.bacc as bacc
    from concourse.bass_utils import run_bass_kernel_spmd

    def arr(name):
        return np.asarray(inputs[name])

    w_xproj = arr("L0_attn_W_xproj")
    w_dt = arr("L0_attn_W_dt")
    inner, dtr = w_dt.shape
    dstate = (w_xproj.shape[0] - dtr) // 2
    w12, w3, gate_w = arr("L0_ffn_w12"), arr("L0_ffn_w3"), arr("L0_ffn_gate_w")
    experts, d, hidden = w3.shape
    nj = dstate * inner // P
    a_log = arr("L0_attn_A_log").T.reshape(nj, P).T
    taps = np.concatenate([arr("L0_attn_Kx")[:, 0, :], arr("L0_attn_Kz")[:, 0, :]], axis=0)
    rank_key = np.broadcast_to(np.arange(experts, 0, -1, dtype=np.float32), (P, 2 * TILES, experts))
    parts = {
        "first": {"ident": np.eye(P, dtype=np.float32), "w_in": arr("L0_attn_W_in").T, "gate": gate_w.T, "a_log": a_log,
                  "rank_key": rank_key.reshape(P, -1)},
        "late": {"taps": taps, "w_out": arr("L0_attn_W_out").T,
                 "wx_bc": np.concatenate([w_xproj[dtr:].T] * 2, axis=0), "b_dt": arr("L0_attn_b_dt")[:, None], "d_skip": arr("L0_attn_D")[:, None],
                 "wx_dt": w_xproj[:dtr], "w_dt": w_dt.T},
    }
    packed, places = {}, {}
    for name, of in parts.items():
        packed[name] = np.zeros((P, sum(a.shape[1] for a in of.values())), np.float32)
        places[name], start = {}, 0
        for key, a in of.items():
            places[name][key] = (a.shape[0], start, start + a.shape[1])
            packed[name][:a.shape[0], start:start + a.shape[1]] = a
            start += a.shape[1]
    arrays = {
        "x": arr("L0_attn_x"),
        "first": packed["first"],
        "late": packed["late"],
        "w12_t": w12.transpose(2, 0, 1),
        "w3_t": w3.reshape(experts, d, hidden // P, P).transpose(3, 0, 2, 1),
    }
    arrays = {k: np.ascontiguousarray(a) for k, a in arrays.items()}
    nc = bacc.Bacc("TRN2", target_bir_lowering=False, num_devices=1)
    ins = {k: nc.dram_tensor(k, a.shape, mybir.dt.from_np(a.dtype), kind="ExternalInput").ap() for k, a in arrays.items()}
    out = nc.dram_tensor("out", arrays["x"].shape, F32, kind="ExternalOutput").ap()
    mixer_moe_kernel(nc, out=out, first_at=places["first"], late_at=places["late"], **ins)
    r = run_bass_kernel_spmd(nc, [arrays], core_ids=[0])
    return r.results[0]["out"]
```
